# Optimizing a Trainium2 kernel written in Bass

```python
import numpy as np
import jax
import jax.numpy as jnp

def _softmax(x, axis=-1):
    return jax.nn.softmax(x, axis=axis)

def _gelu(x):
    return jax.nn.gelu(x, approximate=True)

def _silu(x):
    return jax.nn.silu(x)

def _sigmoid(x):
    return jax.nn.sigmoid(x)

def _layernorm(x, axis=-1, eps=1e-05):
    m = jnp.mean(x, axis=axis, keepdims=True)
    v = jnp.var(x, axis=axis, keepdims=True)
    return (x - m) / jnp.sqrt(v + eps)

def _scatter_add(tgt, idx, src, axis=0):
    return tgt.at[idx].add(src)

def _segment_sum(src, seg, n):
    return jax.ops.segment_sum(src, seg, n)
kernel_name = 'mk_decoder_postln_d1_seqx_r4_f9fe51'

def setup_inputs(seed: int=0):
    np.random.seed(seed)
    _w = jnp.asarray

    def _rec_inputs():
        import jax
        import jax.numpy as jnp
        _rk = jax.random.key(seed)
        x = -0.0003929 + 0.9999 * jax.random.normal(jax.random.fold_in(_rk, 1), (32, 100, 256), jnp.float32)
        _lenS = 100 - jax.random.randint(jax.random.fold_in(_rk, 7), (32,), 0, max(1, 100 // 4) + 1, jnp.int32)
        _lenS2 = 361 - jax.random.randint(jax.random.fold_in(_rk, 8), (32,), 0, max(1, 361 // 4) + 1, jnp.int32)
        _ctx_1024P = jax.random.normal(jax.random.fold_in(_rk, 11), (32, 16, 256), jnp.float32)
        _ctx_1024c = jax.random.dirichlet(jax.random.fold_in(_rk, 511), 0.3 * jnp.ones((16,), jnp.float32), (32, 361))
        _ctx_1024t = jnp.einsum('bsk,bkd->bsd', _ctx_1024c, _ctx_1024P)
        _ctx_1024t = _ctx_1024t * jax.lax.rsqrt(jnp.mean(jnp.square(_ctx_1024t)) + 1e-12) * 0.953939
        ctx_1024 = 2.81802e-05 + 1.00001 * (_ctx_1024t + 0.3 * jax.random.normal(jax.random.fold_in(_rk, 611), (32, 361, 256), jnp.float32))
        _validS = jnp.arange(100)[None, :] < _lenS[:, None]
        _validS2 = jnp.arange(361)[None, :] < _lenS2[:, None]
        _causal = jnp.tril(jnp.ones((100, 100), dtype=bool))
        mask_1xSxS2_ik1 = jnp.where(jnp.broadcast_to(_validS2[0:1, None, :], (1, 100, 361)), 1, 0).astype(jnp.int32)
        return (x, ctx_1024, mask_1xSxS2_ik1)
    x, ctx_1024, mask_1xSxS2_ik1 = _rec_inputs()

    def _L0_attn_setup():
        import jax, jax.numpy as jnp
        import numpy as np
        import math
        B, S, D = (4, 512, 256)
        H = 16
        HD = D // H
        DL = 64
        LAMBDA_DECAY = 0.01
        key = jax.random.key(seed)
        ks = jax.random.split(key, 8)
        sc = lambda fan_in: 1.0 / math.sqrt(fan_in)
        return {'x': jax.random.normal(ks[0], (B, S, D), dtype=jnp.float32), 'W_q': jax.random.normal(ks[1], (D, D), dtype=jnp.float32) * sc(D), 'W_k': jax.random.normal(ks[2], (D, D), dtype=jnp.float32) * sc(D), 'W_v': jax.random.normal(ks[3], (D, D), dtype=jnp.float32) * sc(D), 'W_o': jax.random.normal(ks[4], (D, D), dtype=jnp.float32) * sc(D), 'W_down_kv': jax.random.normal(ks[5], (D, DL), dtype=jnp.float32) * sc(D), 'W_up_k': jax.random.normal(ks[6], (DL, D), dtype=jnp.float32) * sc(DL), 'W_up_v': jax.random.normal(ks[7], (DL, D), dtype=jnp.float32) * sc(DL)}
    _L0_attn_all = _L0_attn_setup()
    _L0_attn_in = {k: v for k, v in _L0_attn_all.items() if k in ('W_q', 'W_k', 'W_v', 'W_o', 'W_down_kv', 'W_up_k', 'W_up_v')}
    del _L0_attn_all

    def _L0_xattn_setup():
        import jax, jax.numpy as jnp
        import numpy as np
        D_MODEL, D_K, D_V = (256, 64, 64)
        B, S = (4, 1024)
        key = jax.random.key(seed)
        ks = jax.random.split(key, 13)
        s = 1.0 / np.sqrt(D_MODEL)
        inp = {'q': jax.random.normal(ks[0], (B, S, D_MODEL), jnp.float32), 'k': jax.random.normal(ks[1], (B, S, D_MODEL), jnp.float32), 'v': jax.random.normal(ks[2], (B, S, D_MODEL), jnp.float32), 'mask': jax.random.randint(ks[3], (1, S, S), 0, 2, jnp.int32), 'Wq': jax.random.normal(ks[4], (D_K, D_MODEL), jnp.float32) * s, 'bq': jax.random.normal(ks[5], (D_K,), jnp.float32) * s, 'Wk': jax.random.normal(ks[6], (D_K, D_MODEL), jnp.float32) * s, 'bk': jax.random.normal(ks[7], (D_K,), jnp.float32) * s, 'Wv': jax.random.normal(ks[8], (D_V, D_MODEL), jnp.float32) * s, 'bv': jax.random.normal(ks[9], (D_V,), jnp.float32) * s, 'Wo': jax.random.normal(ks[10], (D_MODEL, D_V), jnp.float32) / np.sqrt(D_V), 'bo': jax.random.normal(ks[11], (D_MODEL,), jnp.float32) / np.sqrt(D_V)}
        return inp
    _L0_xattn_all = _L0_xattn_setup()
    _L0_xattn_in = {k: v for k, v in _L0_xattn_all.items() if k in ('Wq', 'bq', 'Wk', 'bk', 'Wv', 'bv', 'Wo', 'bo')}
    del _L0_xattn_all

    def _L0_ffn_setup():
        import jax, jax.numpy as jnp
        import numpy as np
        B, S, D, H, E = (8, 512, 256, 1024, 16)
        key = jax.random.key(seed)
        ks = jax.random.split(key, 4)
        sd = 1.0 / np.sqrt(D).astype(np.float32)
        sh = 1.0 / np.sqrt(H).astype(np.float32)
        return {'x': jax.random.normal(ks[0], (B, S, D), jnp.float32), 'Wg': jax.random.normal(ks[1], (D, E), jnp.float32) * sd, 'bg': jnp.zeros((E,), jnp.float32), 'W1': jax.random.normal(ks[2], (E, D, H), jnp.float32) * sd, 'b1': jnp.zeros((E, H), jnp.float32), 'W2': jax.random.normal(ks[3], (E, H, D), jnp.float32) * sh, 'b2': jnp.zeros((E, D), jnp.float32)}
    _L0_ffn_all = _L0_ffn_setup()
    _L0_ffn_in = {k: v for k, v in _L0_ffn_all.items() if k in ('Wg', 'bg', 'W1', 'b1', 'W2', 'b2')}
    del _L0_ffn_all
    return {'x': x, 'ctx_1024': ctx_1024, 'mask_1xSxS2_ik1': mask_1xSxS2_ik1, 'L0_attn_W_q': _L0_attn_in['W_q'], 'L0_attn_W_k': _L0_attn_in['W_k'], 'L0_attn_W_v': _L0_attn_in['W_v'], 'L0_attn_W_o': _L0_attn_in['W_o'], 'L0_attn_W_down_kv': _L0_attn_in['W_down_kv'], 'L0_attn_W_up_k': _L0_attn_in['W_up_k'], 'L0_attn_W_up_v': _L0_attn_in['W_up_v'], 'L0_xattn_Wq': _L0_xattn_in['Wq'], 'L0_xattn_bq': _L0_xattn_in['bq'], 'L0_xattn_Wk': _L0_xattn_in['Wk'], 'L0_xattn_bk': _L0_xattn_in['bk'], 'L0_xattn_Wv': _L0_xattn_in['Wv'], 'L0_xattn_bv': _L0_xattn_in['bv'], 'L0_xattn_Wo': _L0_xattn_in['Wo'], 'L0_xattn_bo': _L0_xattn_in['bo'], 'L0_ffn_Wg': _L0_ffn_in['Wg'], 'L0_ffn_bg': _L0_ffn_in['bg'], 'L0_ffn_W1': _L0_ffn_in['W1'], 'L0_ffn_b1': _L0_ffn_in['b1'], 'L0_ffn_W2': _L0_ffn_in['W2'], 'L0_ffn_b2': _L0_ffn_in['b2']}

def reference(x, ctx_1024, mask_1xSxS2_ik1, L0_attn_W_q, L0_attn_W_k, L0_attn_W_v, L0_attn_W_o, L0_attn_W_down_kv, L0_attn_W_up_k, L0_attn_W_up_v, L0_xattn_Wq, L0_xattn_bq, L0_xattn_Wk, L0_xattn_bk, L0_xattn_Wv, L0_xattn_bv, L0_xattn_Wo, L0_xattn_bo, L0_ffn_Wg, L0_ffn_bg, L0_ffn_W1, L0_ffn_b1, L0_ffn_W2, L0_ffn_b2):
    import jax
    import jax.numpy as jnp

    def _L0_attn_ref(x, W_q, W_k, W_v, W_o, W_down_kv, W_up_k, W_up_v):
        import jax, jax.numpy as jnp
        import numpy as np
        import math
        B, S, D = (4, 512, 256)
        H = 16
        HD = D // H
        DL = 64
        LAMBDA_DECAY = 0.01
        b, s, d = x.shape
        q = x @ W_q
        k = x @ W_k
        v = x @ W_v
        latent_kv = (k + v) @ W_down_kv
        k_rec = (latent_kv @ W_up_k).reshape(b, s, H, HD).transpose(0, 2, 1, 3)
        v_rec = (latent_kv @ W_up_v).reshape(b, s, H, HD).transpose(0, 2, 1, 3)
        qh = q.reshape(b, s, H, HD).transpose(0, 2, 1, 3)
        scores = jnp.einsum('bhqd,bhkd->bhqk', qh, k_rec) / math.sqrt(d)
        t = jnp.arange(s, dtype=jnp.float32)
        decay = jnp.exp(-LAMBDA_DECAY * jnp.abs(t[:, None] - t[None, :]))
        scores = scores * decay[None, None, :, :]
        attn = jax.nn.softmax(scores, axis=-1)
        out = jnp.einsum('bhqk,bhkd->bhqd', attn, v_rec)
        out = out.transpose(0, 2, 1, 3).reshape(b, s, d)
        return out @ W_o

    def _L0_xattn_ref(q, k, v, mask, Wq, bq, Wk, bk, Wv, bv, Wo, bo):
        import jax, jax.numpy as jnp
        import numpy as np
        D_MODEL, D_K, D_V = (256, 64, 64)
        B, S = (4, 1024)
        qh = jnp.einsum('bsd,kd->bsk', q, Wq) + bq
        kh = jnp.einsum('bsd,kd->bsk', k, Wk) + bk
        vh = jnp.einsum('bsd,vd->bsv', v, Wv) + bv
        scale = 1.0 / jnp.sqrt(jnp.float32(D_K))
        scores = jnp.einsum('bqk,bmk->bqm', qh, kh) * scale
        scores = jnp.where(mask == 0, jnp.float32(-1000000000.0), scores)
        attn = jax.nn.softmax(scores, axis=-1)
        out = jnp.einsum('bqm,bmv->bqv', attn, vh)
        return jnp.einsum('bqv,dv->bqd', out, Wo) + bo

    def _L0_ffn_ref(x, Wg, bg, W1, b1, W2, b2):
        import jax, jax.numpy as jnp
        import numpy as np
        B, S, D, H, E = (8, 512, 256, 1024, 16)
        d = x.shape[-1]
        xf = x.reshape(-1, d)
        n_tok = xf.shape[0]
        n_exp = Wg.shape[1]
        cap = -(-n_tok // n_exp)
        score = jax.nn.softmax(xf @ Wg + bg, axis=-1)
        gate = jnp.max(score, axis=-1)
        idx = jnp.argmax(score, axis=-1)
        onehot = jax.nn.one_hot(idx, n_exp, dtype=jnp.int32)
        pos = jnp.sum((jnp.cumsum(onehot, axis=0) - 1) * onehot, axis=-1)
        keep = pos < cap
        safe_pos = jnp.where(keep, pos, cap - 1)
        buf = jnp.zeros((n_exp, cap, d), x.dtype).at[idx, safe_pos].add(jnp.where(keep[:, None], xf, 0.0))
        h = jax.nn.relu(jnp.einsum('ecd,edh->ech', buf, W1) + b1[:, None, :])
        y = jnp.einsum('ech,ehd->ecd', h, W2) + b2[:, None, :]
        out = y[idx, safe_pos] * gate[:, None]
        out = jnp.where(keep[:, None], out, 0.0)
        return out.reshape(x.shape)
    x = _layernorm(x + _L0_attn_ref(x, L0_attn_W_q, L0_attn_W_k, L0_attn_W_v, L0_attn_W_o, L0_attn_W_down_kv, L0_attn_W_up_k, L0_attn_W_up_v), axis=-1)
    x = _layernorm(x + _L0_xattn_ref(x, ctx_1024, ctx_1024, mask_1xSxS2_ik1, L0_xattn_Wq, L0_xattn_bq, L0_xattn_Wk, L0_xattn_bk, L0_xattn_Wv, L0_xattn_bv, L0_xattn_Wo, L0_xattn_bo), axis=-1)
    x = _layernorm(x + _L0_ffn_ref(x, L0_ffn_Wg, L0_ffn_bg, L0_ffn_W1, L0_ffn_b1, L0_ffn_W2, L0_ffn_b2), axis=-1)
    return x

_drawn_inputs = setup_inputs


def setup_inputs(seed=0):
    import zlib

    import numpy as np

    out = dict(_drawn_inputs(seed))
    spreads = {'L0_ffn_bg': (0.0, 0.1), 'L0_ffn_b1': (0.0, 0.467), 'L0_ffn_b2': (0.0, 0.326)}
    factors = {'L0_xattn_bk': 8.0}
    for name, (base, spread) in spreads.items():
        noise = np.random.default_rng([zlib.crc32(name.encode()), seed]).standard_normal(out[name].shape)
        drawn = base * np.exp(spread * noise) if base else spread * noise
        out[name] = jnp.asarray(drawn.astype(out[name].dtype))
    for name, factor in factors.items():
        out[name] = (out[name] * factor).astype(out[name].dtype)
    return out
```

```python
from contextlib import ExitStack

import numpy as np

import concourse.bass as bass
from concourse import mybir

F32 = mybir.dt.float32
I32 = mybir.dt.int32
U32 = mybir.dt.uint32
ALU = mybir.AluOpType
ACT = mybir.ActivationFunctionType
AX_X = mybir.AxisListType.X

P = 128
B, S, D = 32, 100, 256
DC = D // P
H, HD = 16, 16
HQ = 4
Q = H // HQ
DL = 64
M = 361
MT = [(0, 128), (128, 128), (256, 105)]
DK = 64
E, HID = 16, 1024
HC = HID // P
T = B * S
CAP = -(-T // E)
HALF = CAP // 2
ROW = 260
GATE, TOK = D, D + 1
FAR = 1.0e6
MASKED = -1.0e30
EPS = 1e-5
LOOP0, LOOP1 = 4, 14
STEPS = 20

C_ID, C_DEC, C_TRI, C_HM, C_REV, C_TOK = 0, 128, 228, 328, 332, 364
C_ALL = 396


def constants():
    c = np.zeros((P, C_ALL), np.float32)
    i = np.arange(S)
    c[:, C_ID:C_ID + P] = np.eye(P)
    t = i.astype(np.float32)
    c[:S, C_DEC:C_DEC + S] = np.exp(np.float32(-0.01) * np.abs(t[:, None] - t[None, :])) / np.float32(16.0)
    c[:S, C_TRI:C_TRI + S] = i[:, None] <= i[None, :]
    c[:, C_HM:C_HM + HQ] = (np.arange(P)[:, None] % DK) // HD == np.arange(HQ)[None, :]
    c[:, C_REV:C_REV + 2 * E] = np.tile(E - np.arange(E), 2)[None, :]
    c[:S, C_TOK:C_TOK + B] = i[:, None] + S * np.arange(B)[None, :]
    return c


def decoder_kernel(nc, a, out):
    ctx = ExitStack()
    with ctx:
        def sb(name, shape, dt=F32):
            return ctx.enter_context(nc.sbuf_tensor(name, shape, dt))

        def sem(name):
            return ctx.enter_context(nc.semaphore(name))

        bank = [ctx.enter_context(nc.psum_tensor(f"bank{i}", [P, 512], F32)) for i in range(8)]
        psS, psT, psO, M0, M1, M2 = bank[0:2], bank[2:4], bank[4], bank[5], bank[6], bank[7]
        psH, psX, psY = bank[0:4], bank[4], bank[5:7]

        cst = sb("cst", [P, C_ALL])
        ident = cst[:, C_ID:C_ID + P]
        dec = cst[0:S, C_DEC:C_DEC + S]
        tri = cst[0:S, C_TRI:C_TRI + S]
        hm = cst[:, C_HM:C_HM + HQ]
        rev = cst[0:S, C_REV:C_REV + 2 * E].rearrange("p (s e) -> p s e", s=2)
        tok = cst[0:S, C_TOK:C_TOK + B]
        ones = sb("ones", [P, P])
        half = sb("half", [P, 2])
        epst = sb("epst", [P, 2])
        wq = sb("wq", [P, DC, D])
        wkT = sb("wkT", [P, DC, D])
        wvT = sb("wvT", [P, DC, D])
        wd = sb("wd", [P, DC, DL])
        wc = sb("wc", [P, DC, DL])
        wuk = sb("wuk", [DL, D])
        wuv = sb("wuv", [DL, D])
        wo = sb("wo", [P, DC, D])
        xwq = sb("xwq", [P, DC, DK])
        xwkv = sb("xwkv", [P, DC, 2 * DK])
        xbq = sb("xbq", [DK, 1])
        xbkv = sb("xbkv", [2 * DK, 1])
        xwo = sb("xwo", [DK + 1, D])
        wg = sb("wg", [P, DC, E])
        bg = sb("bg", [S, E])
        mski = sb("mski", [S, M], I32)
        msk = sb("msk", [S, M])
        empty = sb("empty", [P, ROW])

        xT = sb("xT", [P, DC, 2 * S])
        xN = sb("xN", [S, 2, D])
        qT = sb("qT", [P, DC, 2 * S])
        latT = sb("latT", [DL, 2 * S])
        kM = sb("kM", [P, 2, DC, HQ, S])
        vS = sb("vS", [S, 2, H, HD + 1])
        sc = sb("sc", [S, H, S])
        mx = sb("mx", [S, H])
        pr = sb("pr", [S, H, S])
        pT = sb("pT", [S, 2, HQ, S])
        rec = sb("rec", [S, H])
        at = sb("at", [S, H, HD])
        aT = sb("aT", [P, DC, S])
        z1 = sb("z1", [S, D])
        st1, mv1, ve1, rs1 = sb("st1", [S, 6]), sb("mv1", [S, 2]), sb("ve1", [S, 1]), sb("rs1", [S, 1])
        x1 = sb("x1", [S, 2, D])

        cT = sb("cT", [P, 2, DC, M])
        x1T = sb("x1T", [P, DC, S])
        qhT = sb("qhT", [DK, S])
        kvT = sb("kvT", [2 * DK, M])
        vh = sb("vh", [P, 2, 3, DK + 1])
        sB = sb("sB", [S, M])
        mxB = sb("mxB", [S, 1])
        nmB = sb("nmB", [S, 1])
        pB = sb("pB", [S, M])
        rsB = sb("rsB", [S, 2])
        rvB = sb("rvB", [S, 1])
        pBT = sb("pBT", [P, 3, S])
        oT = sb("oT", [DK + 1, S])
        z2 = sb("z2", [S, D])
        st2, mv2, ve2, rs2 = sb("st2", [S, 6]), sb("mv2", [S, 2]), sb("ve2", [S, 1]), sb("rs2", [S, 1])
        x2 = sb("x2", [S, 2, D])

        x2T = sb("x2T", [P, DC, S])
        lg = sb("lg", [S, 2, E])
        st3, mv3, ve3, rs3 = sb("st3", [S, 6]), sb("mv3", [S, 2]), sb("ve3", [S, 1]), sb("rs3", [S, 1])
        x3 = sb("x3", [S, 2, D])
        row = sb("row", [S, 2, ROW])
        lmax = sb("lmax", [S, 2])
        ld = sb("ld", [S, 2, E])
        le = sb("le", [S, 2, E])
        key = sb("key", [S, 2, E])
        kmax = sb("kmax", [S, 2])
        oh = sb("oh", [S, 2, E])
        seen = sb("seen", [S, E])
        pose = sb("pose", [S, 2, E])
        pos = sb("pos", [S, 2])
        over = sb("over", [S, 2])
        base = sb("base", [S, 2])
        slot = sb("slot", [S, 2], I32)
        den = sb("den", [S, 2])

        w1 = sb("w1", [P, 2, DC, HID])
        w2 = sb("w2", [P, 2, HC, D])
        b1 = sb("b1", [P, 2, HC])
        b2 = sb("b2", [HALF, 2, D])
        bx = sb("bx", [HALF, 2, 2, ROW])
        bxT = sb("bxT", [P, 2, DC, CAP])
        hT = sb("hT", [P, 2, HC, CAP])
        yb = sb("yb", [HALF, 2, D])
        zf = sb("zf", [HALF, 2, D])
        stf, mvf = sb("stf", [HALF, 2, 6]), sb("mvf", [HALF, 2, 2])
        vef, rsf = sb("vef", [HALF, 2]), sb("rsf", [HALF, 2])
        yo = sb("yo", [HALF, 2, 2, D])
        toki = sb("toki", [HALF, 2, 2], I32)

        slots = nc.dram_tensor("slots", [E * CAP, ROW], F32, kind="Internal").ap()

        l_w, l_xT = sem("l_w"), sem("l_xT")
        l_xN = [sem(f"l_xN{i}") for i in range(2)]
        l_cT = [sem(f"l_cT{i}") for i in range(2)]
        l_w1 = [sem(f"l_w1{i}") for i in range(2)]
        l_w2 = [sem(f"l_w2{i}") for i in range(2)]
        l_bx = [sem(f"l_bx{i}") for i in range(2)]
        s_wc, s_q, s_lat, s_k, s_v, s_S, s_PT, s_PV, s_aT, s_wo = map(
            sem, "s_wc s_q s_lat s_k s_v s_S s_PT s_PV s_aT s_wo".split())
        s_x1T, s_qh, s_kv, s_vh, s_B, s_BT, s_o, s_wo2, s_x2T, s_lg, s_cum = map(
            sem, "s_x1T s_qh s_kv s_vh s_B s_BT s_o s_wo2 s_x2T s_lg s_cum".split())
        s_bT, s_h, s_y = map(sem, "s_bT s_h s_y".split())
        e_q, e_v, e_exp, e_PT, e_aT, e_x1T, e_qh, e_kv, e_vh, e_BT, e_B, e_o, e_x2T, e_le, e_row = map(
            sem, "e_q e_v e_exp e_PT e_aT e_x1T e_qh e_kv e_vh e_BT e_B e_o e_x2T e_le e_row".split())
        e_bT, e_h = map(sem, "e_bT e_h".split())
        d_msk, d_wc, d_lat, d_k, d_mul, d_max, d_rec, d_at, d_z1, d_st1, d_mv1 = map(
            sem, "d_msk d_wc d_lat d_k d_mul d_max d_rec d_at d_z1 d_st1 d_mv1".split())
        d_B, d_nm, d_rv, d_z2, d_st2, d_mv2, d_lg, d_st3, d_mv3 = map(
            sem, "d_B d_nm d_rv d_z2 d_st2 d_mv2 d_lg d_st3 d_mv3".split())
        d_lmax, d_ld, d_key, d_kmax, d_oh, d_pose, d_pos, d_base, d_slot, d_seen, d_den, d_row = map(
            sem, "d_lmax d_ld d_key d_kmax d_oh d_pose d_pos d_base d_slot d_seen d_den d_row".split())
        d_h, d_yb, d_zf, d_stf, d_mvf, d_tok = map(sem, "d_h d_yb d_zf d_stf d_mvf d_tok".split())
        p_sub, p_row0, p_set, p_ve1, p_rs1, p_x1, p_ve2, p_rs2, p_x2, p_ve3, p_rs3, p_x3 = map(
            sem, "p_sub p_row0 p_set p_ve1 p_rs1 p_x1 p_ve2 p_rs2 p_x2 p_ve3 p_rs3 p_x3".split())
        p_vef, p_rsf, p_yo = map(sem, "p_vef p_rsf p_yo".split())
        o_empty = sem("o_empty")
        o_x3 = [sem(f"o_x3{i}") for i in range(2)]
        o_row = [sem(f"o_row{i}") for i in range(2)]
        o_yo = [[sem(f"o_yo{i}{j}") for j in range(2)] for i in range(2)]

        class Step:

            def __init__(self, u, s):
                self.u, self.s = u, s
                self.peeled = isinstance(u, int)

            def live(self, k):
                return not self.peeled or 0 <= 2 * self.u + self.s - k < B

            def at(self, per, k, j):
                return self.u * (2 * per) + (per * (self.s - k) + j)

            def half_at(self, k):
                return self.u * 16 + (((self.s - k) // 2) + 1) * 16

            def par(self, k):
                return (self.s - k) % 2

            def pair_live(self, k):
                return not self.peeled or 0 <= self.u - k < B // 2

            def pair(self, k, per=1, j=1):
                return self.u * per + (j - k * per)

            def batch(self, k):
                return self.u * 2 + (self.s - k)

        def experts(eng, expert):
            for r in range(2):
                expert(0, r, r == 1, False, False)
            with eng.Fori(1, E // 2 - 1) as v:
                for r in range(2):
                    expert(v, r, True, True, False)
            for r in range(2):
                expert(E // 2 - 1, r, True, True, r == 1)

        def turns(eng, step):
            for u in range(LOOP0):
                for s in range(2):
                    step(Step(u, s))
            with eng.Fori(LOOP0, LOOP1) as u:
                for s in range(2):
                    step(Step(u, s))
            for u in range(LOOP1, STEPS):
                for s in range(2):
                    step(Step(u, s))

        N_W = 19
        N_SET = 8

        def waits(eng, *pairs):
            values = [v if isinstance(v, int) else eng.to_reg(v) for _, v in pairs]
            eng.wait_ge(l_w, 16)
            for (s_, _), v in zip(pairs, values):
                eng.wait_ge(s_, v)

        block = ctx.enter_context(nc.Block())

        @block.sync
        def _(sp):
            ctx_v = a["ctxT"].rearrange("(c p) (b m) -> p c b m", p=P, m=M)
            xT_v = a["xT"].rearrange("(c p) t -> p c t", p=P)
            out_v = out.rearrange("b s d -> (b s) d")

            def load_xT(t0):
                sp.dma_start(xT[:, :, :], xT_v[:, :, bass.ds(t0, 2 * S)]).then_inc(l_xT, 16)

            def load_xN(b, i):
                sp.dma_start(xN[:, i, :], a["x"][bass.ds(b, 1), :, :].rearrange("o s d -> (o s) d")).then_inc(l_xN[i], 16)

            def load_cT(b, i):
                sp.dma_start(cT[:, i, :, :], ctx_v[:, :, bass.ds(b, 1), :].rearrange("p c o m -> p c (o m)")).then_inc(l_cT[i], 16)

            def load_w1(e, r):
                sp.dma_start(w1[:, r, :, :], a["w1"][bass.ds(e, 1), :, :].rearrange("o (c p) h -> p (o c) h", p=P)).then_inc(l_w1[r], 16)

            def load_w2(e, r):
                sp.dma_start(w2[:, r, :, :], a["w2"][bass.ds(e, 1), :, :].rearrange("o (c p) h -> p (o c) h", p=P)).then_inc(l_w2[r], 16)

            def load_b1(e, r):
                sp.dma_start(b1[:, r, :], a["b1"][bass.ds(e, 1), :, :].rearrange("o p j -> p (o j)")).then_inc(l_w1[r], 16)

            def load_b2(e, r):
                sp.dma_start(b2[:, r, :], a["b2"][bass.ds(e, 1), :].broadcast_to([HALF, D])).then_inc(l_w2[r], 16)

            def load_bx(e, r):
                sp.dma_start(bx[:, r, :, :], slots[bass.ds(e * CAP, CAP), :].rearrange("(i p) c -> p i c", p=HALF)).then_inc(l_bx[r], 16)

            n = [0]

            def w(dst, src):
                sp.dma_start(dst, src).then_inc(l_w, 16)
                n[0] += 1

            w(cst[:, :], a["cst"])
            w(wkT[:, :, :], a["wkT"].rearrange("(c p) n -> p c n", p=P))
            w(wvT[:, :, :], a["wvT"].rearrange("(c p) n -> p c n", p=P))
            w(wd[:, :, :], a["wd"].rearrange("(c p) n -> p c n", p=P))
            load_xT(0)
            w(wq[:, :, :], a["wq"].rearrange("(c p) n -> p c n", p=P))
            w(wuk[:, :], a["wuk"])
            w(wuv[:, :], a["wuv"])
            load_xN(0, 0)
            load_xN(1, 1)
            load_cT(0, 0)
            load_cT(1, 1)
            w(wo[:, :, :], a["wo"].rearrange("(c p) n -> p c n", p=P))
            w(xwq[:, :, :], a["xwqT"].rearrange("(c p) n -> p c n", p=P))
            w(xwkv[:, :, 0:DK], a["xwkT"].rearrange("(c p) n -> p c n", p=P))
            w(xwkv[:, :, DK:2 * DK], a["xwvT"].rearrange("(c p) n -> p c n", p=P))
            w(xbq[:, :], a["xbq"])
            w(xbkv[0:DK, :], a["xbk"])
            w(xbkv[DK:2 * DK, :], a["xbv"])
            w(xwo[0:DK, :], a["xwoT"])
            w(xwo[DK:DK + 1, :], a["xbo"])
            w(wg[:, :, :], a["wg"].rearrange("(c p) n -> p c n", p=P))
            w(bg[:, :], a["bg"].broadcast_to([S, E]))
            w(mski[:, :], a["mask"])
            sp.wait_ge(p_set, N_SET)
            sp.dma_start(slots.rearrange("(n p) c -> p n c", p=P),
                         empty[:, :].rearrange("p (o c) -> p o c", o=1).broadcast_to([P, E * CAP // P, ROW])).then_inc(o_empty, 16)
            sp.wait_ge(s_k, 1)
            load_xT(2 * S)
            for r in range(2):
                load_w1(r, r)
                load_b1(r, r)
                load_w2(r, r)
                load_b2(r, r)
            assert n[0] == N_W, n[0]

            def step(st):
                s = st.s
                if s == 1 and st.pair_live(-2):
                    sp.wait_ge(s_k, st.pair(-1))
                    load_xT(st.batch(-3) * S)
                if st.live(2) and st.live(0):
                    sp.wait_ge(d_z1, st.at(1, 2, 1))
                    load_xN(st.batch(0), s)
                if st.live(3) and st.live(1):
                    sp.wait_ge(s_kv, st.at(1, 3, 1))
                    load_cT(st.batch(1), st.par(1))
                if st.live(6):
                    sp.wait_ge(p_x3, st.at(1, 6, 1))
                    sp.dma_start(out_v[bass.ds(st.batch(6) * S, S), :], x3[:, st.par(6), :]).then_inc(o_x3[st.par(6)], 16)

            turns(sp, step)
            for i in range(2):
                sp.wait_ge(o_row[i], 16 * (B // 2))
            for r in range(2):
                load_bx(r, r)
            with sp.Fori(0, E // 2 - 1) as v:
                for r in range(2):
                    n1 = v * 2 + (r + 1)
                    waits(sp, (s_h, v * 8 + (4 * r + 4)), (e_h, v * 4 + (2 * r + 2)), (d_h, v * 4 + (2 * r + 2)))
                    load_w1(v * 2 + (2 + r), r)
                    load_b1(v * 2 + (2 + r), r)
                    sp.wait_ge(s_y, n1)
                    load_w2(v * 2 + (2 + r), r)
                    sp.wait_ge(d_zf, v * 4 + (2 * r + 2))
                    load_b2(v * 2 + (2 + r), r)
                    sp.wait_ge(d_tok, n1)
                    load_bx(v * 2 + (2 + r), r)
            for r in range(2):
                for i in range(2):
                    sp.wait_ge(o_yo[r][i], 16 * (E // 2))
                sp.wait_ge(o_x3[r], 16 * (B // 2))

        @block.tensor
        def _(pe):
            mm = pe.matmul

            def wait_latest(*users):
                for there, s_, value in users:
                    if there:
                        pe.wait_ge(s_, value)
                        return

            pe.wait_ge(l_w, 16 * N_W)
            for c in range(DC):
                for w_, first in ((wkT, True), (wvT, False)):
                    for k in range(DC):
                        last = mm(M0[:, c * DL:(c + 1) * DL], w_[:, k, c * P:(c + 1) * P], wd[:, k, :],
                                  start=first and k == 0, stop=not first and k == DC - 1)
            last.then_inc(s_wc, 1)
            pe.wait_ge(d_wc, 1)
            pe.wait_ge(p_set, N_SET)

            def project_latent(p):
                pe.wait_ge(l_xT, p * 16)
                for c in range(DC):
                    i = mm(M1[0:DL, 0:2 * S], wc[:, c, :], xT[:, c, :], start=c == 0, stop=c == DC - 1)
                i.then_inc(s_lat, 1)

            def project_q():
                for o in range(DC):
                    for c in range(DC):
                        i = mm(M2[:, o * 2 * S:(o + 1) * 2 * S], wq[:, c, o * P:(o + 1) * P], xT[:, c, :],
                               start=c == 0, stop=c == DC - 1)
                i.then_inc(s_q, 1)

            def project_k(p):
                pe.wait_ge(d_lat, p)
                for o in range(DC):
                    i = mm(M0[:, o * 2 * S:(o + 1) * 2 * S], wuk[:, o * P:(o + 1) * P], latT[:, :], start=True, stop=True)
                i.then_inc(s_k, 1)

            project_latent(1)
            project_q()
            project_k(1)

            def slot0(st):
                s = st.s
                if st.live(5):
                    pe.wait_ge(e_o, st.at(1, 5, 1))
                    if s == 0 and st.pair_live(0):
                        pe.wait_ge(e_q, st.pair(0))
                    mm(M2[0:S, 0:D], oT[:, :], xwo[:, :], start=True, stop=True).then_inc(s_wo2, 1)
                if s == 0 and st.pair_live(4):
                    pe.wait_ge(d_oh, st.pair(4))
                    wait_latest((st.pair_live(0), d_k, st.pair(0, 2, 2)), (st.live(4), d_B, st.at(1, 4, 1)),
                                (st.live(5), d_B, st.at(1, 5, 1)), (st.pair_live(5), d_pose, st.pair(5)))
                    mm(M0[0:S, 0:2 * E], tri, oh[:, :, :], start=True, stop=False)
                    mm(M0[0:S, 0:2 * E], ones[0:S, 0:S],
                       seen[:, :].rearrange("p (o e) -> p o e", o=1).broadcast_to([S, 2, E]), start=False, stop=False)
                    mm(M0[0:S, E:2 * E], ones[0:S, 0:S], oh[:, 0, :], start=False, stop=True).then_inc(s_cum, 1)
                if st.live(3):
                    pe.wait_ge(l_cT[st.par(3)], st.half_at(3))
                    wait_latest((st.live(5), e_o, st.at(1, 5, 1)), (s == 0 and st.pair_live(0), d_lat, st.pair(0)),
                                (st.live(1), e_v, st.at(1, 1, 1)))
                    for c in range(DC):
                        i = mm(M1[:, 0:M], xwkv[:, c, :], cT[:, st.par(3), c, :], start=c == 0, stop=c == DC - 1)
                    i.then_inc(s_kv, 1)
                if st.live(2):
                    pe.wait_ge(d_at, st.at(1, 2, 1))
                    wait_latest((s == 0 and st.pair_live(4), d_pose, st.pair(4)), (s == 0 and st.pair_live(0), d_k, st.pair(0, 2, 2)),
                                (st.live(4), d_B, st.at(1, 4, 1)), (st.live(3), d_z1, st.at(1, 3, 1)))
                    for c in range(DC):
                        i = pe.transpose(M0[:, c * S:(c + 1) * S], at[:, c * 8:(c + 1) * 8, :], ident[0:S, 0:S])
                    i.then_inc(s_aT, 1)

            def slot1(st):
                if st.live(6):
                    pe.wait_ge(p_x2, st.at(1, 6, 1))
                    wait_latest((st.live(5), d_z2, st.at(1, 5, 1)), (st.live(7), d_lg, st.at(1, 7, 1)))
                    for c in range(DC):
                        i = pe.transpose(M2[:, c * S:(c + 1) * S], x2[:, st.par(6), c * P:(c + 1) * P], ident[0:S, 0:S])
                    i.then_inc(s_x2T, 1)
                if st.live(3):
                    pe.wait_ge(p_x1, st.at(1, 3, 1))
                    pe.wait_ge(e_kv, st.at(1, 3, 1))
                    for c in range(DC):
                        i = pe.transpose(M1[:, c * S:(c + 1) * S], x1[:, st.par(3), c * P:(c + 1) * P], ident[0:S, 0:S])
                    i.then_inc(s_x1T, 1)
                if st.live(2):
                    pe.wait_ge(e_aT, st.at(1, 2, 1))
                    for c in range(DC):
                        i = mm(M0[0:S, 0:D], aT[:, c, :], wo[:, c, :], start=c == 0, stop=c == DC - 1)
                    i.then_inc(s_wo, 1)

            def slot2(st):
                s = st.s
                if st.live(3):
                    pe.wait_ge(e_x1T, st.at(1, 3, 1))
                    wait_latest((st.live(2), d_z1, st.at(1, 2, 1)), (s == 0 and st.pair_live(4), d_pose, st.pair(4)))
                    for c in range(DC):
                        i = mm(M0[0:DK, 0:S], xwq[:, c, :], x1T[:, c, :], start=c == 0, stop=c == DC - 1)
                    i.then_inc(s_qh, 1)
                    for m, (m0, mn) in enumerate(MT):
                        i = pe.transpose(M1[0:mn, m * DK:(m + 1) * DK], kvT[DK:2 * DK, m0:m0 + mn],
                                         ident[DK:2 * DK, DK:2 * DK])
                    i.then_inc(s_vh, 1)
                if st.live(6):
                    pe.wait_ge(e_x2T, st.at(1, 6, 1))
                    for c in range(DC):
                        i = mm(M2[0:S, 0:E], x2T[:, c, :], wg[:, c, :], start=c == 0, stop=c == DC - 1)
                    i.then_inc(s_lg, 1)
                if st.live(0):
                    wait_latest((st.live(3), e_vh, st.at(1, 3, 1)), (s == 0, d_lat, st.pair(0)), (st.live(1), e_v, st.at(1, 1, 1)))
                    mm(M1[0:S, 0:D], latT[:, s * S:(s + 1) * S], wuv[:, :], start=True, stop=True).then_inc(s_v, 1)

            def slot3(st):
                s = st.s
                if st.live(4):
                    pe.wait_ge(e_B, st.at(1, 4, 1))
                    wait_latest((st.live(6), d_lg, st.at(1, 6, 1)), (st.live(5), d_z2, st.at(1, 5, 1)),
                                (st.pair_live(0), e_q, st.pair(0)))
                    for m, (m0, mn) in enumerate(MT):
                        i = pe.transpose(M2[0:mn, m * S:(m + 1) * S], pB[:, m0:m0 + mn], ident[0:S, 0:S])
                    i.then_inc(s_BT, 1)
                if s == 1 and st.pair_live(-1):
                    pe.wait_ge(e_v, st.at(1, 0, 1))
                    project_latent(st.pair(-1))
                if st.live(3):
                    pe.wait_ge(e_qh, st.at(1, 3, 1))
                    mm(M0[0:S, 0:M], qhT[:, :], kvT[0:DK, :], start=True, stop=True).then_inc(s_B, 1)

            def ends(st):
                s = st.s
                if st.live(4):
                    pe.wait_ge(e_BT, st.at(1, 4, 1))
                    wait_latest((s == 1 and st.pair_live(-1), d_lat, st.pair(-1)), (st.live(0), e_v, st.at(1, 0, 1)),
                                (st.live(3), e_vh, st.at(1, 3, 1)), (st.live(5), e_o, st.at(1, 5, 1)))
                    for m, (m0, mn) in enumerate(MT):
                        i = mm(M1[0:DK + 1, 0:S], vh[0:mn, st.par(4), m, :], pBT[0:mn, m, :], start=m == 0, stop=m == 2)
                    i.then_inc(s_o, 1)
                if s == 1 and st.pair_live(-1):
                    project_q()
                    if st.live(3):
                        pe.wait_ge(d_B, st.at(1, 3, 1))
                    project_k(st.pair(-1))

            def step(st):
                s = st.s
                for g, others in enumerate((slot0, slot1, slot2, slot3)):
                    if st.live(1):
                        pe.wait_ge(e_exp, st.at(Q, 1, g + 1))
                        if g >= 2 or st.live(2):
                            pe.wait_ge(e_PT, st.at(Q, 1, g - 1))
                        for j in range(HQ):
                            i = pe.transpose(psT[g % 2][0:S, j * S:(j + 1) * S], pr[:, g * HQ + j, :], ident[0:S, 0:S])
                        i.then_inc(s_PT, 1)
                    others(st)
                    if st.live(0):
                        if g == 0 and s == 0:
                            pe.wait_ge(e_q, st.pair(0))
                            pe.wait_ge(d_k, st.pair(0, 2, 2))
                        if g >= 2 or st.live(1):
                            pe.wait_ge(d_mul, st.at(Q, 0, g - 1))
                        r0 = DK * (g % 2)
                        mm(psS[g % 2][0:S, 0:HQ * S], qT[r0:r0 + DK, g // 2, s * S:(s + 1) * S],
                           kM[r0:r0 + DK, s, g // 2, :, :], start=True, stop=True).then_inc(s_S, 1)
                    if st.live(1):
                        pe.wait_ge(e_PT, st.at(Q, 1, g + 1))
                        if g == 0:
                            pe.wait_ge(e_v, st.at(1, 1, 1))
                            if st.live(2):
                                pe.wait_ge(d_at, st.at(1, 2, 1))
                        for j in range(HQ):
                            h = g * HQ + j
                            i = mm(psO[0:S, h * (HD + 1):(h + 1) * (HD + 1)], pT[:, g % 2, j, :],
                                   vS[:, st.par(1), h, :], start=True, stop=True)
                        i.then_inc(s_PV, 1)
                ends(st)

            turns(pe, step)

            for s_, n in ((d_mul, Q * B), (e_PT, Q * B), (d_at, B), (d_pose, B // 2), (d_B, B), (e_o, B)):
                pe.wait_ge(s_, n)

            def rows_in(r, loaded):
                pe.wait_ge(l_bx[r], loaded)
                for c in range(DC):
                    for i in range(2):
                        k = c * 2 + i
                        ins = pe.transpose(psX[:, k * HALF:(k + 1) * HALF], bx[:, r, i, c * P:(c + 1) * P], ident[0:HALF, 0:HALF])
                ins.then_inc(s_bT, 1)

            rows_in(0, 16)

            def expert(v, r, old1, old2, last):
                n2 = v * 4 + 2 * r
                pe.wait_ge(e_bT, v * 2 + (r + 1))
                pe.wait_ge(l_w1[r], v * 32 + 32)
                for q in range(HC // 2):
                    if old1:
                        pe.wait_ge(e_h if q % 2 == 0 else d_h, n2 + (q // 2 - 1))
                    for j in (2 * q, 2 * q + 1):
                        for c in range(DC):
                            i = mm(psH[q][:, (j % 2) * CAP:(j % 2 + 1) * CAP], w1[:, r, c, j * P:(j + 1) * P],
                                   bxT[:, r, c, :], start=c == 0, stop=c == DC - 1)
                    i.then_inc(s_h, 1)
                if not last:
                    rows_in(1 - r, v * 16 + (16 if r == 0 else 32))
                pe.wait_ge(l_w2[r], v * 32 + 32)
                if old2:
                    pe.wait_ge(d_yb, v * 2 + (r - 1))
                pe.wait_ge(e_h, n2 + 2)
                pe.wait_ge(d_h, n2 + 2)
                for i in range(2):
                    for j in range(HC):
                        ins = mm(psY[r][0:HALF, i * D:(i + 1) * D], hT[:, r, j, i * HALF:(i + 1) * HALF], w2[:, r, j, :],
                                 start=j == 0, stop=j == HC - 1)
                ins.then_inc(s_y, 1)

            experts(pe, expert)

        @block.scalar
        def _(act):
            def copy(dst, src):
                return act.activation(dst, src, ACT.Copy)

            def put_q(p):
                act.wait_ge(s_q, p)
                copy(qT[:, :, :].rearrange("p c t -> p (c t)"), M2[:, 0:DC * 2 * S]).then_inc(e_q, 1)

            def probabilities(st, k, g):
                act.wait_ge(p_sub, st.at(Q, k, g + 1))
                if st.live(k + 1):
                    act.wait_ge(s_PT, st.at(Q, k + 1, g + 1))
                act.activation(pr[:, g * HQ:(g + 1) * HQ, :], sc[:, g * HQ:(g + 1) * HQ, :], ACT.Exp).then_inc(e_exp, 1)

            put_q(1)

            def step(st):
                s = st.s
                for g in range(Q):
                    if st.live(1):
                        act.wait_ge(s_PT, st.at(Q, 1, g + 1))
                        if g >= 2 or st.live(2):
                            act.wait_ge(s_PV, st.at(Q, 1, g - 1))
                        copy(pT[:, g % 2, :, :].rearrange("p h q -> p (h q)"), psT[g % 2][0:S, 0:HQ * S]).then_inc(e_PT, 1)
                    if g == 0:
                        if st.live(3):
                            act.wait_ge(s_kv, st.at(1, 3, 1))
                            if st.live(4):
                                act.wait_ge(s_B, st.at(1, 4, 1))
                            act.activation(kvT[:, :], M1[:, 0:M], ACT.Identity, bias=xbkv[:, :]).then_inc(e_kv, 1)
                        if st.live(2):
                            act.wait_ge(s_aT, st.at(1, 2, 1))
                            if st.live(3):
                                act.wait_ge(s_wo, st.at(1, 3, 1))
                            copy(aT[:, :, :].rearrange("p c q -> p (c q)"), M0[:, 0:DC * S]).then_inc(e_aT, 1)
                        if st.live(1):
                            probabilities(st, 1, Q - 1)
                    if g == 1:
                        if st.live(6):
                            act.wait_ge(s_x2T, st.at(1, 6, 1))
                            copy(x2T[:, :, :].rearrange("p c q -> p (c q)"), M2[:, 0:DC * S]).then_inc(e_x2T, 1)
                        if st.live(3):
                            act.wait_ge(s_x1T, st.at(1, 3, 1))
                            copy(x1T[:, :, :].rearrange("p c q -> p (c q)"), M1[:, 0:DC * S]).then_inc(e_x1T, 1)
                    if g == 2:
                        if st.live(3):
                            act.wait_ge(s_qh, st.at(1, 3, 1))
                            act.activation(qhT[:, :], M0[0:DK, 0:S], ACT.Identity, bias=xbq[:, :]).then_inc(e_qh, 1)
                            act.wait_ge(s_vh, st.at(1, 3, 1))
                            copy(vh[:, st.par(3), 0:2, 0:DK], M1[:, 0:2 * DK].rearrange("p (m d) -> p m d", m=2))
                            copy(vh[0:MT[2][1], st.par(3), 2, 0:DK], M1[0:MT[2][1], 2 * DK:3 * DK]).then_inc(e_vh, 1)
                        if st.live(0):
                            act.wait_ge(s_v, st.at(1, 0, 1))
                            copy(vS[:, s, :, 0:HD], M1[0:S, 0:D].rearrange("p (h d) -> p h d", h=H)).then_inc(e_v, 1)
                    if g == 3 and st.live(4):
                        act.wait_ge(s_BT, st.at(1, 4, 1))
                        copy(pBT[:, 0:2, :].rearrange("p m q -> p (m q)"), M2[:, 0:2 * S])
                        copy(pBT[0:MT[2][1], 2, :], M2[0:MT[2][1], 2 * S:3 * S]).then_inc(e_BT, 1)
                    if g >= 1 and st.live(0):
                        probabilities(st, 0, g - 1)
                if st.live(3):
                    act.wait_ge(d_nm, st.at(1, 3, 1))
                    if st.live(4):
                        act.wait_ge(s_BT, st.at(1, 4, 1))
                    act.activation(pB[:, :], sB[:, :], ACT.Exp, bias=nmB[:, :], scale=0.125,
                                   accum_out=rsB[:, st.par(3):st.par(3) + 1]).then_inc(e_B, 1)
                if st.live(4):
                    act.wait_ge(s_o, st.at(1, 4, 1))
                    copy(oT[:, :], M1[0:DK + 1, 0:S]).then_inc(e_o, 1)
                if st.live(6):
                    if st.live(8):
                        act.wait_ge(o_row[s], st.half_at(8))
                    copy(row[:, s, 0:D], x2[:, s, :]).then_inc(e_row, 1)
                if s == 1 and st.pair_live(-1):
                    put_q(st.pair(-1))
                if s == 1 and st.pair_live(3):
                    act.wait_ge(d_ld, st.pair(3))
                    act.activation(le[:, :, :], ld[:, :, :], ACT.Exp).then_inc(e_le, 1)

            turns(act, step)

            def rows_in(n, r):
                act.wait_ge(s_bT, n)
                copy(bxT[:, r, :, :].rearrange("p c t -> p (c t)"), psX[:, 0:DC * CAP]).then_inc(e_bT, 1)

            rows_in(1, 0)

            def expert(v, r, old1, old2, last):
                act.wait_ge(l_w1[r], v * 32 + 32)
                if old2:
                    act.wait_ge(s_y, v * 2 + (r - 1))
                for q in (0, 2):
                    act.wait_ge(s_h, v * 8 + (4 * r + q + 1))
                    for j in (2 * q, 2 * q + 1):
                        i = act.activation(hT[:, r, j, :], psH[q][:, (j % 2) * CAP:(j % 2 + 1) * CAP], ACT.Relu,
                                           bias=b1[:, r, j:j + 1])
                    i.then_inc(e_h, 1)
                if not last:
                    rows_in(v * 2 + (r + 2), 1 - r)

            experts(act, expert)

        @block.vector
        def _(dve):
            def normal_stats(z, stats, moments, s_z, n_z, s_st, s_mv, value):
                dve.wait_ge(s_z, n_z)
                dve.bn_stats(stats, z).then_inc(s_st, 1)
                waits(dve, (s_st, value))
                dve.bn_aggr(moments, stats).then_inc(s_mv, 1)

            dve.wait_ge(l_w, 16 * N_W)
            dve.tensor_scalar(msk[:, :], mski[:, :], 0.0, MASKED, ALU.is_equal, ALU.mult).then_inc(d_msk, 1)
            dve.wait_ge(s_wc, 1)
            dve.tensor_copy(wc[:, :, :].rearrange("p c l -> p (c l)"), M0[:, 0:DC * DL]).then_inc(d_wc, 1)

            def put_latent(p):
                dve.wait_ge(s_lat, p)
                dve.tensor_copy(latT[:, :], M1[0:DL, 0:2 * S]).then_inc(d_lat, 1)

            def put_keys(p):
                dve.wait_ge(s_k, p)
                for i in range(2):
                    src = M0[:, 0:DC * 2 * S].rearrange("p (c o t) -> p c o t", c=DC, o=1)[:, :, :, i * S:(i + 1) * S]
                    dve.tensor_tensor(kM[:, i, :, :, :], src.broadcast_to([P, DC, HQ, S]),
                                      hm.rearrange("p (o h q) -> p o h q", o=1, q=1).broadcast_to([P, DC, HQ, S]),
                                      ALU.mult).then_inc(d_k, 1)

            put_latent(1)
            put_keys(1)

            def step(st):
                s = st.s
                if st.live(2):
                    dve.wait_ge(s_PV, st.at(Q, 2, Q))
                    o = psO[0:S, 0:H * (HD + 1)].rearrange("p (h d) -> p h d", h=H)
                    dve.reciprocal(rec[:, :].rearrange("p (h o) -> p h o", o=1), o[:, :, HD:HD + 1]).then_inc(d_rec, 1)
                    dve.wait_ge(d_rec, st.at(1, 2, 1))
                    if st.live(3):
                        dve.wait_ge(s_aT, st.at(1, 3, 1))
                    dve.tensor_tensor(at[:, :, :], o[:, :, 0:HD],
                                      rec[:, :].rearrange("p (h o) -> p h o", o=1).broadcast_to([S, H, HD]),
                                      ALU.mult).then_inc(d_at, 1)
                if s == 0 and st.pair_live(4):
                    dve.wait_ge(s_cum, st.pair(4))
                    dve.tensor_tensor(pose[:, :, :], M0[0:S, 0:2 * E].rearrange("p (s e) -> p s e", s=2), oh[:, :, :],
                                      ALU.mult).then_inc(d_pose, 1)
                    dve.tensor_tensor(seen[:, :], seen[:, :], oh[:, 0, :], ALU.add).then_inc(d_seen, 1)
                    dve.wait_ge(d_seen, st.pair(4, 2, 1))
                    dve.tensor_tensor(seen[:, :], seen[:, :], oh[:, 1, :], ALU.add).then_inc(d_seen, 1)
                    dve.wait_ge(d_pose, st.pair(4))
                    dve.tensor_reduce(pos[:, :], pose[:, :, :], AX_X, ALU.add).then_inc(d_pos, 1)
                    dve.wait_ge(d_pos, st.pair(4))
                    dve.tensor_scalar(over[:, :], pos[:, :], float(CAP), FAR, ALU.is_gt, ALU.mult)
                    dve.scalar_tensor_tensor(out=base[:, :], in0=kmax[:, :], scalar=-float(CAP), in1=pos[:, :],
                                             op0=ALU.mult, op1=ALU.add).then_inc(d_base, 1)
                    dve.wait_ge(d_base, st.pair(4))
                    if st.pair_live(5):
                        dve.wait_ge(o_row[1], (st.pair(5)) * 16)
                    dve.scalar_tensor_tensor(out=slot[:, :], in0=base[:, :], scalar=float(E * CAP - 1), in1=over[:, :],
                                             op0=ALU.add, op1=ALU.add).then_inc(d_slot, 1)
                    dve.wait_ge(e_le, st.pair(4))
                    dve.tensor_reduce(den[:, :], le[:, :, :], AX_X, ALU.add).then_inc(d_den, 1)
                    dve.wait_ge(d_den, st.pair(4))
                    dve.wait_ge(e_row, st.pair(4, 2, 2))
                    dve.reciprocal(row[:, :, GATE:GATE + 1], den[:, :].rearrange("p (s o) -> p s o", o=1)).then_inc(d_row, 1)
                    dve.tensor_copy(row[:, :, TOK:TOK + 1],
                                    tok[:, bass.ds(st.batch(8), 2)].rearrange("p (s o) -> p s o", o=1)).then_inc(d_row, 1)
                if st.live(5):
                    dve.wait_ge(e_B, st.at(1, 5, 1))
                    dve.reciprocal(rvB[:, :], rsB[:, st.par(5):st.par(5) + 1]).then_inc(d_rv, 1)
                    dve.wait_ge(d_rv, st.at(1, 5, 1))
                    dve.wait_ge(s_wo2, st.at(1, 5, 1))
                    if st.live(6):
                        dve.wait_ge(p_x2, st.at(1, 6, 1))
                    dve.scalar_tensor_tensor(out=z2[:, :], in0=M2[0:S, 0:D], scalar=rvB[:, :], in1=x1[:, st.par(5), :],
                                             op0=ALU.mult, op1=ALU.add).then_inc(d_z2, 1)
                    normal_stats(z2[:, :], st2[:, :], mv2[:, :], d_z2, st.at(1, 5, 1), d_st2, d_mv2, st.at(1, 5, 1))
                for g in range(Q):
                    if st.live(0):
                        dve.wait_ge(s_S, st.at(Q, 0, g + 1))
                        if st.live(1):
                            dve.wait_ge(e_exp, st.at(Q, 1, g + 1))
                        quad = sc[:, g * HQ:(g + 1) * HQ, :]
                        dve.tensor_tensor(quad, psS[g % 2][0:S, 0:HQ * S].rearrange("p (h k) -> p h k", h=HQ),
                                          dec.rearrange("p (o k) -> p o k", o=1).broadcast_to([S, HQ, S]),
                                          ALU.mult).then_inc(d_mul, 1)
                        dve.wait_ge(d_mul, st.at(Q, 0, g + 1))
                        dve.tensor_reduce(mx[:, g * HQ:(g + 1) * HQ], quad, AX_X, ALU.max).then_inc(d_max, 1)
                    if g == 1 and st.live(2):
                        dve.wait_ge(s_wo, st.at(1, 2, 1))
                        dve.wait_ge(l_xN[st.par(2)], st.half_at(2))
                        if st.live(3):
                            dve.wait_ge(p_x1, st.at(1, 3, 1))
                        dve.tensor_tensor(z1[:, :], M0[0:S, 0:D], xN[:, st.par(2), :], ALU.add).then_inc(d_z1, 1)
                        normal_stats(z1[:, :], st1[:, :], mv1[:, :], d_z1, st.at(1, 2, 1), d_st1, d_mv1, st.at(1, 2, 1))
                    if g == 2 and st.live(6):
                        dve.wait_ge(s_lg, st.at(1, 6, 1))
                        dve.tensor_tensor(lg[:, s, :], M2[0:S, 0:E], bg[:, :], ALU.add).then_inc(d_lg, 1)
                        if st.live(7):
                            dve.wait_ge(p_x3, st.at(1, 7, 1))
                        normal_stats(x2[:, s, :], st3[:, :], mv3[:, :], p_x2, st.at(1, 6, 1), d_st3, d_mv3, st.at(1, 6, 1))
                if s == 1 and st.pair_live(-1):
                    dve.wait_ge(s_v, st.at(1, 0, 1))
                    put_latent(st.pair(-1))
                if st.live(3):
                    waits(dve, (s_B, st.at(1, 3, 1)), *[(e_B, st.at(1, 4, 1))] * st.live(4))
                    dve.tensor_tensor_reduce(sB[:, :], M0[0:S, 0:M], msk[:, :], 1.0, -3.0e38, ALU.add, ALU.max,
                                             mxB[:, :]).then_inc(d_B, 1)
                    dve.wait_ge(d_B, st.at(1, 3, 1))
                    dve.tensor_scalar(nmB[:, :], mxB[:, :], -0.125, None, ALU.mult).then_inc(d_nm, 1)
                if s == 1 and st.pair_live(-1):
                    dve.wait_ge(s_S, st.at(Q, 0, Q))
                    put_keys(st.pair(-1))
                if s == 1 and st.pair_live(3):
                    dve.wait_ge(d_lg, st.pair(3, 2, 2))
                    dve.tensor_reduce(lmax[:, :], lg[:, :, :], AX_X, ALU.max).then_inc(d_lmax, 1)
                    dve.wait_ge(d_lmax, st.pair(3))
                    dve.tensor_tensor(ld[:, :, :], lg[:, :, :],
                                      lmax[:, :].rearrange("p (s o) -> p s o", o=1).broadcast_to([S, 2, E]),
                                      ALU.subtract).then_inc(d_ld, 1)
                    dve.wait_ge(d_ld, st.pair(3))
                    dve.scalar_tensor_tensor(out=key[:, :, :], in0=ld[:, :, :], scalar=0.0, in1=rev,
                                             op0=ALU.is_ge, op1=ALU.mult).then_inc(d_key, 1)
                    dve.wait_ge(d_key, st.pair(3))
                    dve.tensor_reduce(kmax[:, :], key[:, :, :], AX_X, ALU.max).then_inc(d_kmax, 1)
                    dve.wait_ge(d_kmax, st.pair(3))
                    dve.tensor_tensor(oh[:, :, :], rev,
                                      kmax[:, :].rearrange("p (s o) -> p s o", o=1).broadcast_to([S, 2, E]),
                                      ALU.is_equal).then_inc(d_oh, 1)

            turns(dve, step)

            def expert(v, r, old1, old2, last):
                n = v * 2 + (r + 1)
                dve.wait_ge(l_w1[r], v * 32 + 32)
                if old2:
                    dve.wait_ge(s_y, v * 2 + (r - 1))
                for q in (1, 3):
                    dve.wait_ge(s_h, v * 8 + (4 * r + q + 1))
                    for j in (2 * q, 2 * q + 1):
                        i = dve.tensor_scalar(hT[:, r, j, :], psH[q][:, (j % 2) * CAP:(j % 2 + 1) * CAP],
                                              b1[:, r, j:j + 1], 0.0, ALU.add, ALU.max)
                    i.then_inc(d_h, 1)
                dve.wait_ge(l_bx[r], v * 16 + 16)
                if old2:
                    dve.wait_ge(o_yo[r][1], v * 16)
                    dve.wait_ge(o_yo[r][0], v * 16)
                dve.tensor_copy(toki[:, r, :].rearrange("p (i o) -> p i o", o=1), bx[:, r, :, TOK:TOK + 1]).then_inc(d_tok, 1)
                dve.wait_ge(l_w2[r], v * 32 + 32)
                dve.wait_ge(s_y, n)
                if old1:
                    dve.wait_ge(d_zf, v * 4 + 2 * r)
                dve.tensor_tensor(yb[:, :, :], psY[r][0:HALF, :].rearrange("p (i d) -> p i d", i=2),
                                  b2[:, r, :].rearrange("p (o d) -> p o d", o=1).broadcast_to([HALF, 2, D]),
                                  ALU.add).then_inc(d_yb, 1)
                dve.wait_ge(d_yb, n)
                if old1:
                    dve.wait_ge(p_yo, v * 4 + 2 * r)
                for i in range(2):
                    dve.scalar_tensor_tensor(out=zf[:, i, :], in0=yb[:, i, :], scalar=bx[:, r, i, GATE:GATE + 1],
                                             in1=bx[:, r, i, 0:D], op0=ALU.mult, op1=ALU.add).then_inc(d_zf, 1)
                for i in range(2):
                    dve.wait_ge(d_zf, v * 4 + (2 * r + 1 + i))
                    dve.bn_stats(stf[:, i, :], zf[:, i, :]).then_inc(d_stf, 1)
                for i in range(2):
                    waits(dve, (d_stf, v * 4 + (2 * r + 1 + i)))
                    dve.bn_aggr(mvf[:, i, :], stf[:, i, :]).then_inc(d_mvf, 1)

            experts(dve, expert)

        @block.gpsimd
        def _(pool):
            pool.memset(ones[:, :], 1.0).then_inc(p_set, 1)
            pool.memset(half[:, :], -0.5).then_inc(p_set, 1)
            pool.memset(epst[:, :], EPS).then_inc(p_set, 1)
            pool.memset(seen[:, :], 0.0).then_inc(p_set, 1)
            pool.memset(vS[:, :, :, HD:HD + 1], 1.0).then_inc(p_set, 1)
            pool.memset(vh[:, :, :, DK:DK + 1], 1.0).then_inc(p_set, 1)
            pool.memset(empty[:, 0:TOK], 0.0).then_inc(p_set, 1)
            pool.memset(empty[:, TOK:ROW], FAR).then_inc(p_set, 1)
            pool.memset(row[:, :, TOK + 1:ROW], 0.0).then_inc(p_row0, 1)
            pool.wait_ge(p_set, N_SET)

            def normalise(dst, z, mv, ve, rs, s_mv, s_ve, s_rs, s_x, value):
                pool.wait_ge(s_mv, value)
                pool.tensor_tensor(ve[:, :], mv[:, 1:2], epst[0:S, 0:1], ALU.add).then_inc(s_ve, 1)
                pool.wait_ge(s_ve, value)
                pool.tensor_tensor(rs[:, :], ve[:, :], half[0:S, 0:1], ALU.pow).then_inc(s_rs, 1)
                waits(pool, (s_rs, value))
                pool.tensor_scalar(dst, z, mv[:, 0:1], rs[:, 0:1], ALU.subtract, ALU.mult).then_inc(s_x, 1)

            def step(st):
                s = st.s
                for g in range(Q):
                    if g == 0 and st.live(3):
                        if st.live(5):
                            pool.wait_ge(d_z2, st.at(1, 5, 1))
                        normalise(x1[:, st.par(3), :], z1[:, :], mv1, ve1, rs1, d_mv1, p_ve1, p_rs1, p_x1, st.at(1, 3, 1))
                    if g == 1 and st.live(5):
                        if st.live(7):
                            pool.wait_ge(e_row, st.at(1, 7, 1))
                        normalise(x2[:, st.par(5), :], z2[:, :], mv2, ve2, rs2, d_mv2, p_ve2, p_rs2, p_x2, st.at(1, 5, 1))
                    if g == 3 and st.live(6):
                        if st.live(8):
                            pool.wait_ge(o_x3[s], st.half_at(8))
                        normalise(x3[:, s, :], x2[:, s, :], mv3, ve3, rs3, d_mv3, p_ve3, p_rs3, p_x3, st.at(1, 6, 1))
                    if st.live(0):
                        pool.wait_ge(d_max, st.at(Q, 0, g + 1))
                        quad = sc[:, g * HQ:(g + 1) * HQ, :]
                        pool.tensor_tensor(quad, quad,
                                           mx[:, g * HQ:(g + 1) * HQ].rearrange("p (h o) -> p h o", o=1).broadcast_to([S, HQ, S]),
                                           ALU.subtract).then_inc(p_sub, 1)
                    if g == 2 and s == 0 and st.pair_live(4):
                        waits(pool, (d_row, st.pair(4, 2, 2)), (d_slot, st.pair(4)), (o_empty, 16), (p_row0, 1))
                        for i in range(2):
                            pool.indirect_dma_start(slots, bass.IndirectOffsetOnAxis(ap=slot[:, i:i + 1].bitcast(U32), axis=0),
                                                    row[:, i, :], None, bounds_check=E * CAP - 1,
                                                    oob_is_err=False).then_inc(o_row[i], 16)

            turns(pool, step)

            out_v = out.rearrange("b s d -> (b s) d")
            for i in range(2):
                pool.wait_ge(o_x3[i], 16 * (B // 2))

            def expert(v, r, old1, old2, last):
                m = v * 4 + 2 * r
                n = v * 2 + (r + 1)
                pool.wait_ge(d_mvf, m + 2)
                pool.tensor_tensor(vef[:, :].rearrange("p (i o) -> p i o", o=1), mvf[:, :, 1:2],
                                   epst[0:HALF, 0:2].rearrange("p (i o) -> p i o", o=1), ALU.add).then_inc(p_vef, 1)
                pool.wait_ge(p_vef, n)
                pool.tensor_tensor(rsf[:, :], vef[:, :], half[0:HALF, 0:2], ALU.pow).then_inc(p_rsf, 1)
                for i in range(2):
                    waits(pool, (p_rsf, n), *[(o_yo[r][i], v * 16)] * old2)
                    pool.tensor_scalar(yo[:, r, i, :], zf[:, i, :], mvf[:, i, 0:1], rsf[:, i:i + 1],
                                       ALU.subtract, ALU.mult).then_inc(p_yo, 1)
                pool.wait_ge(d_tok, n)
                for i in range(2):
                    waits(pool, (p_yo, m + (1 + i)))
                    pool.indirect_dma_start(out_v, bass.IndirectOffsetOnAxis(ap=toki[:, r, i:i + 1].bitcast(U32), axis=0),
                                            yo[:, r, i, :], None, bounds_check=T - 1,
                                            oob_is_err=False).then_inc(o_yo[r][i], 16)

            experts(pool, expert)


def layout(x, ctx_1024, mask_1xSxS2_ik1, L0_attn_W_q, L0_attn_W_k, L0_attn_W_v, L0_attn_W_o, L0_attn_W_down_kv,
           L0_attn_W_up_k, L0_attn_W_up_v, L0_xattn_Wq, L0_xattn_bq, L0_xattn_Wk, L0_xattn_bk, L0_xattn_Wv,
           L0_xattn_bv, L0_xattn_Wo, L0_xattn_bo, L0_ffn_Wg, L0_ffn_bg, L0_ffn_W1, L0_ffn_b1, L0_ffn_W2, L0_ffn_b2):
    r = {
        "x": x, "xT": x.transpose(2, 0, 1).reshape(D, T), "ctxT": ctx_1024.transpose(2, 0, 1).reshape(D, B * M),
        "mask": mask_1xSxS2_ik1[0], "wq": L0_attn_W_q, "wkT": L0_attn_W_k.T, "wvT": L0_attn_W_v.T,
        "wo": L0_attn_W_o, "wd": L0_attn_W_down_kv, "wuk": L0_attn_W_up_k, "wuv": L0_attn_W_up_v,
        "xwqT": L0_xattn_Wq.T, "xbq": L0_xattn_bq[:, None], "xwkT": L0_xattn_Wk.T, "xbk": L0_xattn_bk[:, None],
        "xwvT": L0_xattn_Wv.T, "xbv": L0_xattn_bv[:, None], "xwoT": L0_xattn_Wo.T, "xbo": L0_xattn_bo[None, :],
        "wg": L0_ffn_Wg, "bg": L0_ffn_bg[None, :], "w1": L0_ffn_W1,
        "b1": L0_ffn_b1.reshape(E, HC, P).transpose(0, 2, 1), "w2": L0_ffn_W2, "b2": L0_ffn_b2,
        "cst": constants(),
    }
    return {k: np.ascontiguousarray(v) for k, v in r.items()}


def kernel(**inputs):
    import concourse.bacc as bacc
    from concourse.bass_utils import run_bass_kernel_spmd

    arrays = layout(**{k: np.asarray(v) for k, v in inputs.items()})
    nc = bacc.Bacc("TRN2", target_bir_lowering=False, num_devices=1)
    aps = {k: nc.dram_tensor(f"in_{k}", v.shape, mybir.dt.from_np(v.dtype), kind="ExternalInput").ap()
           for k, v in arrays.items()}
    out = nc.dram_tensor("out_0", (B, S, D), F32, kind="ExternalOutput").ap()
    decoder_kernel(nc, aps, out)
    r = run_bass_kernel_spmd(nc, [{f"in_{k}": v for k, v in arrays.items()}], core_ids=[0])
    return r.results[0]["out_0"]
```

```python
from contextlib import ExitStack

import numpy as np

import concourse.bass as bass
from concourse import mybir

F32 = mybir.dt.float32
I32 = mybir.dt.int32
U32 = mybir.dt.uint32
ALU = mybir.AluOpType
ACT = mybir.ActivationFunctionType
AX_X = mybir.AxisListType.X

P = 128
B, S, D = 32, 100, 256
DC = D // P
H, HD = 16, 16
HQ = 4
HP = P // HD
Q = H // HQ
STRIP = P // HQ
DL = 64
M = 361
MT = [(0, 128), (128, 128), (256, 105)]
DK = 64
E, HID = 16, 1024
HC = HID // P
T = B * S
CAP = -(-T // E)
HALF = CAP // 2
ROW = 260
GATE, TOK = D, D + 1
FAR = 1.0e6
MASKED = -1.0e30
EPS = 1e-5
LOOP0, LOOP1 = 4, 14
STEPS = 20

C_ID, C_DEC, C_TRI, C_HM, C_REV, C_TOK = 0, 128, 228, 328, 336, 368
C_ALL = 400


def constants():
    c = np.zeros((P, C_ALL), np.float32)
    i = np.arange(S)
    c[:, C_ID:C_ID + P] = np.eye(P)
    t = i.astype(np.float32)
    c[:S, C_DEC:C_DEC + S] = np.exp(np.float32(-0.01) * np.abs(t[:, None] - t[None, :])) / np.float32(16.0)
    c[:S, C_TRI:C_TRI + S] = i[:, None] <= i[None, :]
    c[:, C_HM:C_HM + HP] = np.arange(P)[:, None] // HD == np.arange(HP)[None, :]
    c[:, C_REV:C_REV + 2 * E] = np.tile(E - np.arange(E), 2)[None, :]
    c[:S, C_TOK:C_TOK + B] = i[:, None] + S * np.arange(B)[None, :]
    return c


def decoder_kernel(nc, a, out):
    ctx = ExitStack()
    with ctx:
        def sb(name, shape, dt=F32):
            return ctx.enter_context(nc.sbuf_tensor(name, shape, dt))

        def sem(name):
            return ctx.enter_context(nc.semaphore(name))

        bank = [ctx.enter_context(nc.psum_tensor(f"bank{i}", [P, 512], F32)) for i in range(8)]
        psS, psT, psO, M0, M1, M2 = bank[0:2], bank[2:4], bank[4], bank[5], bank[6], bank[7]
        psH, psX, psY = bank[0:4], bank[4], bank[5:7]

        cst = sb("cst", [P, C_ALL])
        ident = cst[:, C_ID:C_ID + P]
        dec = cst[0:S, C_DEC:C_DEC + S]
        tri = cst[0:S, C_TRI:C_TRI + S]
        hm = cst[:, C_HM:C_HM + HP]
        rev = cst[0:S, C_REV:C_REV + 2 * E].rearrange("p (s e) -> p s e", s=2)
        tok = cst[0:S, C_TOK:C_TOK + B]
        ones = sb("ones", [P, P])
        half = sb("half", [P, 2])
        epst = sb("epst", [P, 2])
        wq = sb("wq", [P, DC, D])
        wkT = sb("wkT", [P, DC, D])
        wvT = sb("wvT", [P, DC, D])
        wd = sb("wd", [P, DC, DL])
        wc = sb("wc", [P, DC, DL])
        wuk = sb("wuk", [DL, D])
        wuv = sb("wuv", [DL, D])
        wo = sb("wo", [P, DC, D])
        xwq = sb("xwq", [P, DC, DK])
        xwkv = sb("xwkv", [P, DC, 2 * DK])
        xbq = sb("xbq", [DK, 1])
        xbkv = sb("xbkv", [2 * DK, 1])
        xwo = sb("xwo", [DK + 1, D])
        wg = sb("wg", [P, DC, E])
        bg = sb("bg", [S, E])
        mski = sb("mski", [S, M], I32)
        msk = sb("msk", [S, M])
        empty = sb("empty", [P, ROW])

        xT = sb("xT", [P, DC, 2 * S])
        xN = sb("xN", [S, 2, D])
        qT = sb("qT", [P, DC, 2 * S])
        latT = sb("latT", [DL, 2 * S])
        kM = sb("kM", [P, 2, DC, HP, S])
        vS = sb("vS", [S, 2, H, STRIP])
        onesS = sb("onesS", [S, 2, STRIP])
        sc = sb("sc", [S, H, S])
        mx = sb("mx", [S, H])
        pr = sb("pr", [S, H, S])
        pT = sb("pT", [S, 2, HQ, S])
        rec = sb("rec", [P, DC * S])
        aT = sb("aT", [P, DC, S])
        z1 = sb("z1", [S, D])
        st1, mv1, ve1, rs1 = sb("st1", [S, 6]), sb("mv1", [S, 2]), sb("ve1", [S, 1]), sb("rs1", [S, 1])
        x1 = sb("x1", [S, 2, D])

        cT = sb("cT", [P, 2, DC, M])
        x1T = sb("x1T", [P, DC, S])
        qhT = sb("qhT", [DK, S])
        kvT = sb("kvT", [2 * DK, M])
        vh = sb("vh", [P, 2, 3, DK + 1])
        sB = sb("sB", [S, M])
        mxB = sb("mxB", [S, 1])
        nmB = sb("nmB", [S, 1])
        pB = sb("pB", [S, M])
        rsB = sb("rsB", [S, 2])
        rvB = sb("rvB", [S, 1])
        pBT = sb("pBT", [P, 3, S])
        oT = sb("oT", [DK + 1, S])
        z2 = sb("z2", [S, D])
        st2, mv2, ve2, rs2 = sb("st2", [S, 6]), sb("mv2", [S, 2]), sb("ve2", [S, 1]), sb("rs2", [S, 1])
        x2 = sb("x2", [S, 2, D])

        x2T = sb("x2T", [P, DC, S])
        lg = sb("lg", [S, 2, E])
        st3, mv3, ve3, rs3 = sb("st3", [S, 6]), sb("mv3", [S, 2]), sb("ve3", [S, 1]), sb("rs3", [S, 1])
        x3 = sb("x3", [S, 2, D])
        row = sb("row", [S, 2, ROW])
        lmax = sb("lmax", [S, 2])
        ld = sb("ld", [S, 2, E])
        le = sb("le", [S, 2, E])
        key = sb("key", [S, 2, E])
        kmax = sb("kmax", [S, 2])
        oh = sb("oh", [S, 2, E])
        seen = sb("seen", [S, E])
        pose = sb("pose", [S, 2, E])
        pos = sb("pos", [S, 2])
        over = sb("over", [S, 2])
        base = sb("base", [S, 2])
        slot = sb("slot", [S, 2], I32)
        den = sb("den", [S, 2])

        w1 = sb("w1", [P, 2, DC, HID])
        w2 = sb("w2", [P, 2, HC, D])
        b1 = sb("b1", [P, 2, HC])
        b2 = sb("b2", [HALF, 2, D])
        bx = sb("bx", [HALF, 2, 2, ROW])
        bxT = sb("bxT", [P, 2, DC, CAP])
        hT = sb("hT", [P, 2, HC, CAP])
        yb = sb("yb", [HALF, 2, D])
        zf = sb("zf", [HALF, 2, D])
        stf, mvf = sb("stf", [HALF, 2, 6]), sb("mvf", [HALF, 2, 2])
        vef, rsf = sb("vef", [HALF, 2]), sb("rsf", [HALF, 2])
        yo = sb("yo", [HALF, 2, 2, D])
        toki = sb("toki", [HALF, 2, 2], I32)

        slots = nc.dram_tensor("slots", [E * CAP, ROW], F32, kind="Internal").ap()

        l_w, l_xT = sem("l_w"), sem("l_xT")
        l_xN = [sem(f"l_xN{i}") for i in range(2)]
        l_cT = [sem(f"l_cT{i}") for i in range(2)]
        l_w1 = [sem(f"l_w1{i}") for i in range(2)]
        l_w2 = [sem(f"l_w2{i}") for i in range(2)]
        l_bx = [sem(f"l_bx{i}") for i in range(2)]
        s_wc, s_q, s_lat, s_k, s_v, s_S, s_PT, s_PV, s_wo = map(
            sem, "s_wc s_q s_lat s_k s_v s_S s_PT s_PV s_wo".split())
        s_x1T, s_qh, s_kv, s_vh, s_B, s_BT, s_o, s_wo2, s_x2T, s_lg, s_cum = map(
            sem, "s_x1T s_qh s_kv s_vh s_B s_BT s_o s_wo2 s_x2T s_lg s_cum".split())
        s_bT, s_h, s_y = map(sem, "s_bT s_h s_y".split())
        e_q, e_v, e_exp, e_PT, e_x1T, e_qh, e_kv, e_vh, e_BT, e_B, e_o, e_x2T, e_le, e_row = map(
            sem, "e_q e_v e_exp e_PT e_x1T e_qh e_kv e_vh e_BT e_B e_o e_x2T e_le e_row".split())
        e_bT, e_h = map(sem, "e_bT e_h".split())
        d_msk, d_wc, d_lat, d_k, d_mul, d_max, d_rec, d_aT, d_z1, d_st1, d_mv1 = map(
            sem, "d_msk d_wc d_lat d_k d_mul d_max d_rec d_aT d_z1 d_st1 d_mv1".split())
        d_B, d_nm, d_rv, d_z2, d_st2, d_mv2, d_lg, d_st3, d_mv3 = map(
            sem, "d_B d_nm d_rv d_z2 d_st2 d_mv2 d_lg d_st3 d_mv3".split())
        d_lmax, d_ld, d_key, d_kmax, d_oh, d_pose, d_pos, d_base, d_slot, d_seen, d_den, d_row = map(
            sem, "d_lmax d_ld d_key d_kmax d_oh d_pose d_pos d_base d_slot d_seen d_den d_row".split())
        d_h, d_yb, d_zf, d_stf, d_mvf, d_tok = map(sem, "d_h d_yb d_zf d_stf d_mvf d_tok".split())
        p_sub, p_row0, p_set, p_ve1, p_rs1, p_x1, p_ve2, p_rs2, p_x2, p_ve3, p_rs3, p_x3 = map(
            sem, "p_sub p_row0 p_set p_ve1 p_rs1 p_x1 p_ve2 p_rs2 p_x2 p_ve3 p_rs3 p_x3".split())
        p_vef, p_rsf, p_yo = map(sem, "p_vef p_rsf p_yo".split())
        o_empty = sem("o_empty")
        o_x3 = [sem(f"o_x3{i}") for i in range(2)]
        o_row = [sem(f"o_row{i}") for i in range(2)]
        o_yo = [[sem(f"o_yo{i}{j}") for j in range(2)] for i in range(2)]

        class Step:

            def __init__(self, u, s):
                self.u, self.s = u, s
                self.peeled = isinstance(u, int)

            def live(self, k):
                return not self.peeled or 0 <= 2 * self.u + self.s - k < B

            def at(self, per, k, j):
                return self.u * (2 * per) + (per * (self.s - k) + j)

            def half_at(self, k):
                return self.u * 16 + (((self.s - k) // 2) + 1) * 16

            def par(self, k):
                return (self.s - k) % 2

            def pair_live(self, k):
                return not self.peeled or 0 <= self.u - k < B // 2

            def pair(self, k, per=1, j=1):
                return self.u * per + (j - k * per)

            def batch(self, k):
                return self.u * 2 + (self.s - k)

        def experts(eng, expert):
            for r in range(2):
                expert(0, r, r == 1, False, False)
            with eng.Fori(1, E // 2 - 1) as v:
                for r in range(2):
                    expert(v, r, True, True, False)
            for r in range(2):
                expert(E // 2 - 1, r, True, True, r == 1)

        def turns(eng, step):
            for u in range(LOOP0):
                for s in range(2):
                    step(Step(u, s))
            with eng.Fori(LOOP0, LOOP1) as u:
                for s in range(2):
                    step(Step(u, s))
            for u in range(LOOP1, STEPS):
                for s in range(2):
                    step(Step(u, s))

        N_W = 19
        N_SET = 11

        def waits(eng, *pairs):
            values = [v if isinstance(v, int) else eng.to_reg(v) for _, v in pairs]
            eng.wait_ge(l_w, 16)
            for (s_, _), v in zip(pairs, values):
                eng.wait_ge(s_, v)

        block = ctx.enter_context(nc.Block())

        @block.sync
        def _(sp):
            ctx_v = a["ctxT"].rearrange("(c p) (b m) -> p c b m", p=P, m=M)
            xT_v = a["xT"].rearrange("(c p) t -> p c t", p=P)
            out_v = out.rearrange("b s d -> (b s) d")

            def load_xT(t0):
                sp.dma_start(xT[:, :, :], xT_v[:, :, bass.ds(t0, 2 * S)]).then_inc(l_xT, 16)

            def load_xN(b, i):
                sp.dma_start(xN[:, i, :], a["x"][bass.ds(b, 1), :, :].rearrange("o s d -> (o s) d")).then_inc(l_xN[i], 16)

            def load_cT(b, i):
                sp.dma_start(cT[:, i, :, :], ctx_v[:, :, bass.ds(b, 1), :].rearrange("p c o m -> p c (o m)")).then_inc(l_cT[i], 16)

            def load_w1(e, r):
                sp.dma_start(w1[:, r, :, :], a["w1"][bass.ds(e, 1), :, :].rearrange("o (c p) h -> p (o c) h", p=P)).then_inc(l_w1[r], 16)

            def load_w2(e, r):
                sp.dma_start(w2[:, r, :, :], a["w2"][bass.ds(e, 1), :, :].rearrange("o (c p) h -> p (o c) h", p=P)).then_inc(l_w2[r], 16)

            def load_b1(e, r):
                sp.dma_start(b1[:, r, :], a["b1"][bass.ds(e, 1), :, :].rearrange("o p j -> p (o j)")).then_inc(l_w1[r], 16)

            def load_b2(e, r):
                sp.dma_start(b2[:, r, :], a["b2"][bass.ds(e, 1), :].broadcast_to([HALF, D])).then_inc(l_w2[r], 16)

            def load_bx(e, r):
                sp.dma_start(bx[:, r, :, :], slots[bass.ds(e * CAP, CAP), :].rearrange("(i p) c -> p i c", p=HALF)).then_inc(l_bx[r], 16)

            n = [0]

            def w(dst, src):
                sp.dma_start(dst, src).then_inc(l_w, 16)
                n[0] += 1

            w(cst[:, :], a["cst"])
            w(wkT[:, :, :], a["wkT"].rearrange("(c p) n -> p c n", p=P))
            w(wvT[:, :, :], a["wvT"].rearrange("(c p) n -> p c n", p=P))
            w(wd[:, :, :], a["wd"].rearrange("(c p) n -> p c n", p=P))
            load_xT(0)
            w(wq[:, :, :], a["wq"].rearrange("(c p) n -> p c n", p=P))
            w(wuk[:, :], a["wuk"])
            w(wuv[:, :], a["wuv"])
            load_xN(0, 0)
            load_xN(1, 1)
            load_cT(0, 0)
            load_cT(1, 1)
            w(wo[:, :, :], a["wo"].rearrange("(c p) n -> p c n", p=P))
            w(xwq[:, :, :], a["xwqT"].rearrange("(c p) n -> p c n", p=P))
            w(xwkv[:, :, 0:DK], a["xwkT"].rearrange("(c p) n -> p c n", p=P))
            w(xwkv[:, :, DK:2 * DK], a["xwvT"].rearrange("(c p) n -> p c n", p=P))
            w(xbq[:, :], a["xbq"])
            w(xbkv[0:DK, :], a["xbk"])
            w(xbkv[DK:2 * DK, :], a["xbv"])
            w(xwo[0:DK, :], a["xwoT"])
            w(xwo[DK:DK + 1, :], a["xbo"])
            w(wg[:, :, :], a["wg"].rearrange("(c p) n -> p c n", p=P))
            w(bg[:, :], a["bg"].broadcast_to([S, E]))
            w(mski[:, :], a["mask"])
            sp.wait_ge(p_set, N_SET)
            sp.dma_start(slots.rearrange("(n p) c -> p n c", p=P),
                         empty[:, :].rearrange("p (o c) -> p o c", o=1).broadcast_to([P, E * CAP // P, ROW])).then_inc(o_empty, 16)
            sp.wait_ge(s_k, 1)
            load_xT(2 * S)
            for r in range(2):
                load_w1(r, r)
                load_b1(r, r)
                load_w2(r, r)
                load_b2(r, r)
            assert n[0] == N_W, n[0]

            def step(st):
                s = st.s
                if s == 1 and st.pair_live(-2):
                    sp.wait_ge(s_k, st.pair(-1))
                    load_xT(st.batch(-3) * S)
                if st.live(2) and st.live(0):
                    sp.wait_ge(d_z1, st.at(1, 2, 1))
                    load_xN(st.batch(0), s)
                if st.live(3) and st.live(1):
                    sp.wait_ge(s_kv, st.at(1, 3, 1))
                    load_cT(st.batch(1), st.par(1))
                if st.live(6):
                    sp.wait_ge(p_x3, st.at(1, 6, 1))
                    sp.dma_start(out_v[bass.ds(st.batch(6) * S, S), :], x3[:, st.par(6), :]).then_inc(o_x3[st.par(6)], 16)

            turns(sp, step)
            for i in range(2):
                sp.wait_ge(o_row[i], 16 * (B // 2))
            for r in range(2):
                load_bx(r, r)
            with sp.Fori(0, E // 2 - 1) as v:
                for r in range(2):
                    n1 = v * 2 + (r + 1)
                    waits(sp, (s_h, v * 8 + (4 * r + 4)), (e_h, v * 4 + (2 * r + 2)), (d_h, v * 4 + (2 * r + 2)))
                    load_w1(v * 2 + (2 + r), r)
                    load_b1(v * 2 + (2 + r), r)
                    sp.wait_ge(s_y, n1)
                    load_w2(v * 2 + (2 + r), r)
                    sp.wait_ge(d_zf, v * 4 + (2 * r + 2))
                    load_b2(v * 2 + (2 + r), r)
                    sp.wait_ge(d_tok, n1)
                    load_bx(v * 2 + (2 + r), r)
            for r in range(2):
                for i in range(2):
                    sp.wait_ge(o_yo[r][i], 16 * (E // 2))
                sp.wait_ge(o_x3[r], 16 * (B // 2))

        @block.tensor
        def _(pe):
            mm = pe.matmul

            def wait_latest(*users):
                for there, s_, value in users:
                    if there:
                        pe.wait_ge(s_, value)
                        return

            pe.wait_ge(l_w, 16 * N_W)
            for c in range(DC):
                for w_, first in ((wkT, True), (wvT, False)):
                    for k in range(DC):
                        last = mm(M0[:, c * DL:(c + 1) * DL], w_[:, k, c * P:(c + 1) * P], wd[:, k, :],
                                  start=first and k == 0, stop=not first and k == DC - 1)
            last.then_inc(s_wc, 1)
            pe.wait_ge(d_wc, 1)
            pe.wait_ge(p_set, N_SET)

            def project_latent(p):
                pe.wait_ge(l_xT, p * 16)
                for c in range(DC):
                    i = mm(M1[0:DL, 0:2 * S], wc[:, c, :], xT[:, c, :], start=c == 0, stop=c == DC - 1)
                i.then_inc(s_lat, 1)

            def project_q():
                for o in range(DC):
                    for c in range(DC):
                        i = mm(M2[:, o * 2 * S:(o + 1) * 2 * S], wq[:, c, o * P:(o + 1) * P], xT[:, c, :],
                               start=c == 0, stop=c == DC - 1)
                i.then_inc(s_q, 1)

            def project_k(p):
                pe.wait_ge(d_lat, p)
                for o in range(DC):
                    i = mm(M0[:, o * 2 * S:(o + 1) * 2 * S], wuk[:, o * P:(o + 1) * P], latT[:, :], start=True, stop=True)
                i.then_inc(s_k, 1)

            project_latent(1)
            project_q()
            project_k(1)

            def project_v(st, bank_):
                mm(bank_[0:S, 0:D], latT[:, st.s * S:(st.s + 1) * S], wuv[:, :], start=True, stop=True).then_inc(s_v, 1)

            def slot0(st):
                s = st.s
                if s == 1 and st.live(0):
                    wait_latest((st.live(4), d_B, st.at(1, 4, 1)), (st.live(3), d_z1, st.at(1, 3, 1)),
                                (st.live(0), d_k, st.pair(0, 2, 2)))
                    project_v(st, M0)
                if st.live(5):
                    pe.wait_ge(e_o, st.at(1, 5, 1))
                    wait_latest((s == 0 and st.pair_live(0), e_q, st.pair(0)), (st.live(5), e_BT, st.at(1, 5, 1)))
                    mm(M2[0:S, 0:D], oT[:, :], xwo[:, :], start=True, stop=True).then_inc(s_wo2, 1)
                if st.live(3):
                    pe.wait_ge(l_cT[st.par(3)], st.half_at(3))
                    wait_latest((st.live(5), e_o, st.at(1, 5, 1)), (s == 0 and st.pair_live(0), d_lat, st.pair(0)),
                                (st.live(1), e_v, st.at(1, 1, 1)))
                    for c in range(DC):
                        i = mm(M1[:, 0:M], xwkv[:, c, :], cT[:, st.par(3), c, :], start=c == 0, stop=c == DC - 1)
                    i.then_inc(s_kv, 1)

            def slot1(st):
                s = st.s
                if st.live(2):
                    pe.wait_ge(d_aT, st.at(1, 2, 1))
                    wait_latest((s == 1 and st.live(0), e_v, st.at(1, 0, 1)),
                                (s == 0 and st.pair_live(0), d_k, st.pair(0, 2, 2)),
                                (st.live(4), d_B, st.at(1, 4, 1)), (st.live(3), d_z1, st.at(1, 3, 1)))
                    for c in range(DC):
                        i = mm(M0[0:S, 0:D], aT[:, c, :], wo[:, c, :], start=c == 0, stop=c == DC - 1)
                    i.then_inc(s_wo, 1)
                if st.live(6):
                    pe.wait_ge(p_x2, st.at(1, 6, 1))
                    wait_latest((st.live(5), d_z2, st.at(1, 5, 1)), (s == 1 and st.pair_live(4), d_pose, st.pair(4)),
                                (st.live(7), d_lg, st.at(1, 7, 1)))
                    for c in range(DC):
                        i = pe.transpose(M2[:, c * S:(c + 1) * S], x2[:, st.par(6), c * P:(c + 1) * P], ident[0:S, 0:S])
                    i.then_inc(s_x2T, 1)
                if st.live(3):
                    pe.wait_ge(p_x1, st.at(1, 3, 1))
                    pe.wait_ge(e_kv, st.at(1, 3, 1))
                    for c in range(DC):
                        i = pe.transpose(M1[:, c * S:(c + 1) * S], x1[:, st.par(3), c * P:(c + 1) * P], ident[0:S, 0:S])
                    i.then_inc(s_x1T, 1)

            def slot2(st):
                s = st.s
                if st.live(3):
                    waits(pe, (e_x1T, st.at(1, 3, 1)))
                    for m, (m0, mn) in enumerate(MT):
                        i = pe.transpose(M1[0:mn, m * DK:(m + 1) * DK], kvT[DK:2 * DK, m0:m0 + mn],
                                         ident[DK:2 * DK, DK:2 * DK])
                    i.then_inc(s_vh, 1)
                    wait_latest((st.live(2), d_z1, st.at(1, 2, 1)), (True, d_B, st.at(1, 4, 1)))
                    for c in range(DC):
                        i = mm(M0[0:DK, 0:S], xwq[:, c, :], x1T[:, c, :], start=c == 0, stop=c == DC - 1)
                    i.then_inc(s_qh, 1)
                if s == 0 and st.pair_live(4):
                    pe.wait_ge(d_oh, st.pair(4))
                    wait_latest((st.live(6), e_x2T, st.at(1, 6, 1)), (st.live(5), d_z2, st.at(1, 5, 1)),
                                (st.live(7), d_lg, st.at(1, 7, 1)), (st.pair_live(5), d_pose, st.pair(5)))
                    places = M2[0:S, E:3 * E]
                    mm(places, tri, oh[:, :, :], start=True, stop=False)
                    mm(places, ones[0:S, 0:S],
                       seen[:, :].rearrange("p (o e) -> p o e", o=1).broadcast_to([S, 2, E]), start=False, stop=False)
                    mm(M2[0:S, 2 * E:3 * E], ones[0:S, 0:S], oh[:, 0, :], start=False, stop=True).then_inc(s_cum, 1)
                if st.live(6):
                    pe.wait_ge(e_x2T, st.at(1, 6, 1))
                    for c in range(DC):
                        i = mm(M2[0:S, 0:E], x2T[:, c, :], wg[:, c, :], start=c == 0, stop=c == DC - 1)
                    i.then_inc(s_lg, 1)

            def slot3(st):
                s = st.s
                if s == 1 and st.pair_live(-1):
                    wait_latest((st.live(3), e_vh, st.at(1, 3, 1)), (st.live(1), e_v, st.at(1, 1, 1)))
                    project_latent(st.pair(-1))
                if s == 0 and st.live(0):
                    wait_latest((st.live(3), e_vh, st.at(1, 3, 1)), (True, d_lat, st.pair(0)))
                    project_v(st, M1)
                if st.live(4):
                    pe.wait_ge(e_B, st.at(1, 4, 1))
                    wait_latest((s == 0 and st.pair_live(4), d_pose, st.pair(4)), (st.live(6), d_lg, st.at(1, 6, 1)), (st.live(5), d_z2, st.at(1, 5, 1)),
                                (st.pair_live(0), e_q, st.pair(0)))
                    for m, (m0, mn) in enumerate(MT):
                        i = pe.transpose(M2[0:mn, m * S:(m + 1) * S], pB[:, m0:m0 + mn], ident[0:S, 0:S])
                    i.then_inc(s_BT, 1)
                if st.live(3):
                    pe.wait_ge(e_qh, st.at(1, 3, 1))
                    mm(M0[0:S, 0:M], qhT[:, :], kvT[0:DK, :], start=True, stop=True).then_inc(s_B, 1)

            def ends(st):
                s = st.s
                if st.live(4):
                    pe.wait_ge(e_BT, st.at(1, 4, 1))
                if s == 1 and st.pair_live(-1):
                    if not st.live(4):
                        pe.wait_ge(e_q, st.pair(0))
                    project_q()
                if st.live(4):
                    wait_latest((s == 1 and st.pair_live(-1), d_lat, st.pair(-1)), (s == 0 and st.live(0), e_v, st.at(1, 0, 1)),
                                (st.live(3), e_vh, st.at(1, 3, 1)), (st.live(5), e_o, st.at(1, 5, 1)))
                    for m, (m0, mn) in enumerate(MT):
                        i = mm(M1[0:DK + 1, 0:S], vh[0:mn, st.par(4), m, :], pBT[0:mn, m, :], start=m == 0, stop=m == 2)
                    i.then_inc(s_o, 1)
                if s == 1 and st.pair_live(-1):
                    wait_latest((st.live(3), d_B, st.at(1, 3, 1)), (True, e_v, st.at(1, 0, 1)))
                    project_k(st.pair(-1))

            def step(st):
                s = st.s
                for g, others in enumerate((slot0, slot1, slot2, slot3)):
                    if st.live(1):
                        pe.wait_ge(e_exp, st.at(Q, 1, g + 1))
                        if g >= 2 or st.live(2):
                            pe.wait_ge(e_PT, st.at(Q, 1, g - 1))
                        for j in range(HQ):
                            i = pe.transpose(psT[g % 2][0:S, j * S:(j + 1) * S], pr[:, g * HQ + j, :], ident[0:S, 0:S])
                        i.then_inc(s_PT, 1)
                    first = g == 0 and s == 0
                    if first:
                        others(st)
                    if st.live(0):
                        if g == 0:
                            if s == 0:
                                pe.wait_ge(e_q, st.pair(0))
                            pe.wait_ge(d_k, st.pair(0, 2, 1 + s))
                        if g >= 2 or st.live(1):
                            pe.wait_ge(d_mul, st.at(Q, 0, g - 1))
                        h0 = HQ * (g % 2)
                        mm(psS[g % 2][0:S, 0:HQ * S], qT[:, g // 2, s * S:(s + 1) * S],
                           kM[:, s, g // 2, h0:h0 + HQ, :], start=True, stop=True).then_inc(s_S, 1)
                    if not first:
                        others(st)
                    if st.live(1):
                        pe.wait_ge(e_PT, st.at(Q, 1, g + 1))
                        if g == 0:
                            pe.wait_ge(e_v, st.at(1, 1, 1))
                            if st.live(2):
                                pe.wait_ge(d_aT, st.at(1, 2, 1))
                        for k in range(2):
                            for j in range(HQ):
                                rows = slice(j * STRIP, (j + 1) * STRIP)
                                cols = slice((k * DC + g // 2) * S, (k * DC + g // 2 + 1) * S)
                                of = vS[:, st.par(1), g * HQ + j, :] if k == 0 else onesS[:, g % 2, :]
                                i = mm(psO[rows, cols], of, pT[:, g % 2, j, :], start=g == k == 0, stop=g == Q - 1 and k == 1,
                                       tile_position=(0, j * STRIP))
                        i.then_inc(s_PV, 1)
                ends(st)

            turns(pe, step)

            for s_, n in ((d_mul, Q * B), (e_PT, Q * B), (d_aT, B), (d_pose, B // 2), (d_B, B), (e_o, B)):
                pe.wait_ge(s_, n)

            def rows_in(r, loaded):
                pe.wait_ge(l_bx[r], loaded)
                for c in range(DC):
                    for i in range(2):
                        k = c * 2 + i
                        ins = pe.transpose(psX[:, k * HALF:(k + 1) * HALF], bx[:, r, i, c * P:(c + 1) * P], ident[0:HALF, 0:HALF])
                ins.then_inc(s_bT, 1)

            rows_in(0, 16)

            def expert(v, r, old1, old2, last):
                n2 = v * 4 + 2 * r
                pe.wait_ge(e_bT, v * 2 + (r + 1))
                pe.wait_ge(l_w1[r], v * 32 + 32)
                for q in range(HC // 2):
                    if old1:
                        pe.wait_ge(e_h if q % 2 == 0 else d_h, n2 + (q // 2 - 1))
                    for j in (2 * q, 2 * q + 1):
                        for c in range(DC):
                            i = mm(psH[q][:, (j % 2) * CAP:(j % 2 + 1) * CAP], w1[:, r, c, j * P:(j + 1) * P],
                                   bxT[:, r, c, :], start=c == 0, stop=c == DC - 1)
                    i.then_inc(s_h, 1)
                if not last:
                    rows_in(1 - r, v * 16 + (16 if r == 0 else 32))
                pe.wait_ge(l_w2[r], v * 32 + 32)
                if old2:
                    pe.wait_ge(d_yb, v * 2 + (r - 1))
                pe.wait_ge(e_h, n2 + 2)
                pe.wait_ge(d_h, n2 + 2)
                for i in range(2):
                    for j in range(HC):
                        ins = mm(psY[r][0:HALF, i * D:(i + 1) * D], hT[:, r, j, i * HALF:(i + 1) * HALF], w2[:, r, j, :],
                                 start=j == 0, stop=j == HC - 1)
                ins.then_inc(s_y, 1)

            experts(pe, expert)

        @block.scalar
        def _(act):
            def copy(dst, src):
                return act.activation(dst, src, ACT.Copy)

            def put_q(p):
                act.wait_ge(s_q, p)
                copy(qT[:, :, :].rearrange("p c t -> p (c t)"), M2[:, 0:DC * 2 * S]).then_inc(e_q, 1)

            def put_v(st, bank_):
                act.wait_ge(s_v, st.at(1, 0, 1))
                for k in range(2):
                    i = copy(vS[:, st.s, :, :].rearrange("p (c k j) w -> p c k j w", c=DC, k=2)[:, :, k, :, k * HD:(k + 1) * HD],
                             bank_[0:S, 0:D].rearrange("p (c k j d) -> p c k j d", c=DC, k=2, j=HQ)[:, :, k, :, :])
                i.then_inc(e_v, 1)

            def probabilities(st, k, g):
                act.wait_ge(p_sub, st.at(Q, k, g + 1))
                if st.live(k + 1):
                    act.wait_ge(s_PT, st.at(Q, k + 1, g + 1))
                act.activation(pr[:, g * HQ:(g + 1) * HQ, :], sc[:, g * HQ:(g + 1) * HQ, :], ACT.Exp).then_inc(e_exp, 1)

            put_q(1)

            def step(st):
                s = st.s
                for g in range(Q):
                    if st.live(1):
                        act.wait_ge(s_PT, st.at(Q, 1, g + 1))
                        if g >= 2 or st.live(2):
                            act.wait_ge(s_PV, st.at(Q, 1, g - 1))
                        copy(pT[:, g % 2, :, :].rearrange("p h q -> p (h q)"), psT[g % 2][0:S, 0:HQ * S]).then_inc(e_PT, 1)
                    if g == 0:
                        if s == 1 and st.live(0):
                            put_v(st, M0)
                        if st.live(3):
                            act.wait_ge(s_kv, st.at(1, 3, 1))
                            if st.live(4):
                                act.wait_ge(s_B, st.at(1, 4, 1))
                            act.activation(kvT[:, :], M1[:, 0:M], ACT.Identity, bias=xbkv[:, :]).then_inc(e_kv, 1)
                        if st.live(1):
                            probabilities(st, 1, Q - 1)
                    if g == 1:
                        if st.live(6):
                            act.wait_ge(s_x2T, st.at(1, 6, 1))
                            copy(x2T[:, :, :].rearrange("p c q -> p (c q)"), M2[:, 0:DC * S]).then_inc(e_x2T, 1)
                        if st.live(3):
                            act.wait_ge(s_x1T, st.at(1, 3, 1))
                            copy(x1T[:, :, :].rearrange("p c q -> p (c q)"), M1[:, 0:DC * S]).then_inc(e_x1T, 1)
                        if st.live(7):
                            if st.live(9):
                                act.wait_ge(o_row[st.par(7)], st.half_at(9))
                            copy(row[:, st.par(7), 0:D], x2[:, st.par(7), :]).then_inc(e_row, 1)
                    if g == 2:
                        if st.live(3):
                            act.wait_ge(s_vh, st.at(1, 3, 1))
                            copy(vh[:, st.par(3), 0:2, 0:DK], M1[:, 0:2 * DK].rearrange("p (m d) -> p m d", m=2))
                            copy(vh[0:MT[2][1], st.par(3), 2, 0:DK], M1[0:MT[2][1], 2 * DK:3 * DK]).then_inc(e_vh, 1)
                            act.wait_ge(s_qh, st.at(1, 3, 1))
                            act.activation(qhT[:, :], M0[0:DK, 0:S], ACT.Identity, bias=xbq[:, :]).then_inc(e_qh, 1)
                    if g == 3:
                        if s == 0 and st.live(0):
                            put_v(st, M1)
                        if st.live(4):
                            act.wait_ge(s_BT, st.at(1, 4, 1))
                            copy(pBT[:, 0:2, :].rearrange("p m q -> p (m q)"), M2[:, 0:2 * S])
                            copy(pBT[0:MT[2][1], 2, :], M2[0:MT[2][1], 2 * S:3 * S]).then_inc(e_BT, 1)
                    if g >= 1 and st.live(0):
                        probabilities(st, 0, g - 1)
                if s == 1 and st.pair_live(-1):
                    put_q(st.pair(-1))
                if st.live(3):
                    act.wait_ge(d_nm, st.at(1, 3, 1))
                    if st.live(4):
                        act.wait_ge(s_BT, st.at(1, 4, 1))
                    act.activation(pB[:, :], sB[:, :], ACT.Exp, bias=nmB[:, :], scale=0.125,
                                   accum_out=rsB[:, st.par(3):st.par(3) + 1]).then_inc(e_B, 1)
                if st.live(4):
                    act.wait_ge(s_o, st.at(1, 4, 1))
                    copy(oT[:, :], M1[0:DK + 1, 0:S]).then_inc(e_o, 1)
                if s == 1 and st.pair_live(3):
                    act.wait_ge(d_ld, st.pair(3))
                    act.activation(le[:, :, :], ld[:, :, :], ACT.Exp).then_inc(e_le, 1)

            turns(act, step)

            def rows_in(n, r):
                act.wait_ge(s_bT, n)
                copy(bxT[:, r, :, :].rearrange("p c t -> p (c t)"), psX[:, 0:DC * CAP]).then_inc(e_bT, 1)

            rows_in(1, 0)

            def expert(v, r, old1, old2, last):
                act.wait_ge(l_w1[r], v * 32 + 32)
                if old2:
                    act.wait_ge(s_y, v * 2 + (r - 1))
                for q in (0, 2):
                    act.wait_ge(s_h, v * 8 + (4 * r + q + 1))
                    for j in (2 * q, 2 * q + 1):
                        i = act.activation(hT[:, r, j, :], psH[q][:, (j % 2) * CAP:(j % 2 + 1) * CAP], ACT.Relu,
                                           bias=b1[:, r, j:j + 1])
                    i.then_inc(e_h, 1)
                if not last:
                    rows_in(v * 2 + (r + 2), 1 - r)

            experts(act, expert)

        @block.vector
        def _(dve):
            def normal_stats(z, stats, moments, s_z, n_z, s_st, s_mv, value):
                dve.wait_ge(s_z, n_z)
                dve.bn_stats(stats, z).then_inc(s_st, 1)
                waits(dve, (s_st, value))
                dve.bn_aggr(moments, stats).then_inc(s_mv, 1)

            dve.wait_ge(l_w, 16 * N_W)
            dve.tensor_scalar(msk[:, :], mski[:, :], 0.0, MASKED, ALU.is_equal, ALU.mult).then_inc(d_msk, 1)
            dve.wait_ge(s_wc, 1)
            dve.tensor_copy(wc[:, :, :].rearrange("p c l -> p (c l)"), M0[:, 0:DC * DL]).then_inc(d_wc, 1)

            def put_latent(p):
                dve.wait_ge(s_lat, p)
                dve.tensor_copy(latT[:, :], M1[0:DL, 0:2 * S]).then_inc(d_lat, 1)

            def put_keys(p):
                dve.wait_ge(s_k, p)
                for i in range(2):
                    src = M0[:, 0:DC * 2 * S].rearrange("p (c o t) -> p c o t", c=DC, o=1)[:, :, :, i * S:(i + 1) * S]
                    dve.tensor_tensor(kM[:, i, :, :, :], src.broadcast_to([P, DC, HP, S]),
                                      hm.rearrange("p (o h q) -> p o h q", o=1, q=1).broadcast_to([P, DC, HP, S]),
                                      ALU.mult).then_inc(d_k, 1)

            put_latent(1)
            put_keys(1)

            def step(st):
                s = st.s
                if st.live(5):
                    dve.wait_ge(e_B, st.at(1, 5, 1))
                    dve.reciprocal(rvB[:, :], rsB[:, st.par(5):st.par(5) + 1]).then_inc(d_rv, 1)
                    dve.wait_ge(d_rv, st.at(1, 5, 1))
                    dve.wait_ge(s_wo2, st.at(1, 5, 1))
                    if st.live(6):
                        dve.wait_ge(p_x2, st.at(1, 6, 1))
                    dve.scalar_tensor_tensor(out=z2[:, :], in0=M2[0:S, 0:D], scalar=rvB[:, :], in1=x1[:, st.par(5), :],
                                             op0=ALU.mult, op1=ALU.add).then_inc(d_z2, 1)
                    normal_stats(z2[:, :], st2[:, :], mv2[:, :], d_z2, st.at(1, 5, 1), d_st2, d_mv2, st.at(1, 5, 1))
                for g in range(Q):
                    if st.live(0):
                        dve.wait_ge(s_S, st.at(Q, 0, g + 1))
                        if st.live(1):
                            dve.wait_ge(e_exp, st.at(Q, 1, g + 1))
                        quad = sc[:, g * HQ:(g + 1) * HQ, :]
                        dve.tensor_tensor(quad, psS[g % 2][0:S, 0:HQ * S].rearrange("p (h k) -> p h k", h=HQ),
                                          dec.rearrange("p (o k) -> p o k", o=1).broadcast_to([S, HQ, S]),
                                          ALU.mult).then_inc(d_mul, 1)
                        dve.wait_ge(d_mul, st.at(Q, 0, g + 1))
                        dve.tensor_reduce(mx[:, g * HQ:(g + 1) * HQ], quad, AX_X, ALU.max).then_inc(d_max, 1)
                    if g == 1 and st.live(2):
                        dve.wait_ge(s_wo, st.at(1, 2, 1))
                        dve.wait_ge(l_xN[st.par(2)], st.half_at(2))
                        if st.live(3):
                            dve.wait_ge(p_x1, st.at(1, 3, 1))
                        dve.tensor_tensor(z1[:, :], M0[0:S, 0:D], xN[:, st.par(2), :], ALU.add).then_inc(d_z1, 1)
                        normal_stats(z1[:, :], st1[:, :], mv1[:, :], d_z1, st.at(1, 2, 1), d_st1, d_mv1, st.at(1, 2, 1))
                    if g == 2 and st.live(6):
                        dve.wait_ge(s_lg, st.at(1, 6, 1))
                        dve.tensor_tensor(lg[:, s, :], M2[0:S, 0:E], bg[:, :], ALU.add).then_inc(d_lg, 1)
                        if st.live(7):
                            dve.wait_ge(p_x3, st.at(1, 7, 1))
                        normal_stats(x2[:, s, :], st3[:, :], mv3[:, :], p_x2, st.at(1, 6, 1), d_st3, d_mv3, st.at(1, 6, 1))
                    if g == 2 and s == 0 and st.pair_live(4):
                        dve.wait_ge(s_cum, st.pair(4))
                        dve.tensor_tensor(pose[:, :, :], M2[0:S, E:3 * E].rearrange("p (s e) -> p s e", s=2), oh[:, :, :],
                                          ALU.mult).then_inc(d_pose, 1)
                        dve.tensor_tensor(seen[:, :], seen[:, :], oh[:, 0, :], ALU.add).then_inc(d_seen, 1)
                        dve.wait_ge(d_seen, st.pair(4, 2, 1))
                        dve.tensor_tensor(seen[:, :], seen[:, :], oh[:, 1, :], ALU.add).then_inc(d_seen, 1)
                        dve.wait_ge(d_pose, st.pair(4))
                        dve.tensor_reduce(pos[:, :], pose[:, :, :], AX_X, ALU.add).then_inc(d_pos, 1)
                        dve.wait_ge(d_pos, st.pair(4))
                        dve.tensor_scalar(over[:, :], pos[:, :], float(CAP), FAR, ALU.is_gt, ALU.mult)
                        dve.scalar_tensor_tensor(out=base[:, :], in0=kmax[:, :], scalar=-float(CAP), in1=pos[:, :],
                                                 op0=ALU.mult, op1=ALU.add).then_inc(d_base, 1)
                        dve.wait_ge(d_base, st.pair(4))
                        if st.pair_live(5):
                            for i in range(2):
                                dve.wait_ge(o_row[i], (st.pair(5)) * 16)
                        dve.scalar_tensor_tensor(out=slot[:, :], in0=base[:, :], scalar=float(E * CAP - 1), in1=over[:, :],
                                                 op0=ALU.add, op1=ALU.add).then_inc(d_slot, 1)
                        dve.wait_ge(e_le, st.pair(4))
                        dve.tensor_reduce(den[:, :], le[:, :, :], AX_X, ALU.add).then_inc(d_den, 1)
                        dve.wait_ge(d_den, st.pair(4))
                        dve.wait_ge(e_row, st.pair(4, 2, 2))
                        dve.reciprocal(row[:, :, GATE:GATE + 1], den[:, :].rearrange("p (s o) -> p s o", o=1)).then_inc(d_row, 1)
                        dve.tensor_copy(row[:, :, TOK:TOK + 1],
                                        tok[:, bass.ds(st.batch(8), 2)].rearrange("p (s o) -> p s o", o=1)).then_inc(d_row, 1)
                if s == 1 and st.pair_live(-1):
                    dve.wait_ge(s_v, st.at(1, 0, 1))
                    put_latent(st.pair(-1))
                if st.live(3):
                    waits(dve, (s_B, st.at(1, 3, 1)), *[(e_B, st.at(1, 4, 1))] * st.live(4))
                    dve.tensor_tensor_reduce(sB[:, :], M0[0:S, 0:M], msk[:, :], 1.0, -3.0e38, ALU.add, ALU.max,
                                             mxB[:, :]).then_inc(d_B, 1)
                    dve.wait_ge(d_B, st.at(1, 3, 1))
                    dve.tensor_scalar(nmB[:, :], mxB[:, :], -0.125, None, ALU.mult).then_inc(d_nm, 1)
                if st.live(1):
                    dve.wait_ge(s_PV, st.at(Q, 1, Q))
                    dve.reciprocal(rec[:, :], psO[:, DC * S:2 * DC * S]).then_inc(d_rec, 1)
                    dve.wait_ge(d_rec, st.at(1, 1, 1))
                    if st.live(2):
                        dve.wait_ge(s_wo, st.at(1, 2, 1))
                    dve.tensor_tensor(aT[:, :, :].rearrange("p c q -> p (c q)"), psO[:, 0:DC * S], rec[:, :],
                                      ALU.mult).then_inc(d_aT, 1)
                if s == 1 and st.pair_live(3):
                    dve.wait_ge(d_lg, st.pair(3, 2, 2))
                    dve.tensor_reduce(lmax[:, :], lg[:, :, :], AX_X, ALU.max).then_inc(d_lmax, 1)
                    dve.wait_ge(d_lmax, st.pair(3))
                    dve.tensor_tensor(ld[:, :, :], lg[:, :, :],
                                      lmax[:, :].rearrange("p (s o) -> p s o", o=1).broadcast_to([S, 2, E]),
                                      ALU.subtract).then_inc(d_ld, 1)
                    dve.wait_ge(d_ld, st.pair(3))
                    dve.scalar_tensor_tensor(out=key[:, :, :], in0=ld[:, :, :], scalar=0.0, in1=rev,
                                             op0=ALU.is_ge, op1=ALU.mult).then_inc(d_key, 1)
                    dve.wait_ge(d_key, st.pair(3))
                    dve.tensor_reduce(kmax[:, :], key[:, :, :], AX_X, ALU.max).then_inc(d_kmax, 1)
                    dve.wait_ge(d_kmax, st.pair(3))
                    dve.tensor_tensor(oh[:, :, :], rev,
                                      kmax[:, :].rearrange("p (s o) -> p s o", o=1).broadcast_to([S, 2, E]),
                                      ALU.is_equal).then_inc(d_oh, 1)
                if s == 1 and st.pair_live(-1):
                    dve.wait_ge(s_S, st.at(Q, 0, Q))
                    put_keys(st.pair(-1))

            turns(dve, step)

            def expert(v, r, old1, old2, last):
                n = v * 2 + (r + 1)
                dve.wait_ge(l_w1[r], v * 32 + 32)
                if old2:
                    dve.wait_ge(s_y, v * 2 + (r - 1))
                for q in (1, 3):
                    dve.wait_ge(s_h, v * 8 + (4 * r + q + 1))
                    for j in (2 * q, 2 * q + 1):
                        i = dve.tensor_scalar(hT[:, r, j, :], psH[q][:, (j % 2) * CAP:(j % 2 + 1) * CAP],
                                              b1[:, r, j:j + 1], 0.0, ALU.add, ALU.max)
                    i.then_inc(d_h, 1)
                dve.wait_ge(l_bx[r], v * 16 + 16)
                if old2:
                    dve.wait_ge(o_yo[r][1], v * 16)
                    dve.wait_ge(o_yo[r][0], v * 16)
                dve.tensor_copy(toki[:, r, :].rearrange("p (i o) -> p i o", o=1), bx[:, r, :, TOK:TOK + 1]).then_inc(d_tok, 1)
                dve.wait_ge(l_w2[r], v * 32 + 32)
                dve.wait_ge(s_y, n)
                if old1:
                    dve.wait_ge(d_zf, v * 4 + 2 * r)
                dve.tensor_tensor(yb[:, :, :], psY[r][0:HALF, :].rearrange("p (i d) -> p i d", i=2),
                                  b2[:, r, :].rearrange("p (o d) -> p o d", o=1).broadcast_to([HALF, 2, D]),
                                  ALU.add).then_inc(d_yb, 1)
                dve.wait_ge(d_yb, n)
                if old1:
                    dve.wait_ge(p_yo, v * 4 + 2 * r)
                for i in range(2):
                    dve.scalar_tensor_tensor(out=zf[:, i, :], in0=yb[:, i, :], scalar=bx[:, r, i, GATE:GATE + 1],
                                             in1=bx[:, r, i, 0:D], op0=ALU.mult, op1=ALU.add).then_inc(d_zf, 1)
                for i in range(2):
                    dve.wait_ge(d_zf, v * 4 + (2 * r + 1 + i))
                    dve.bn_stats(stf[:, i, :], zf[:, i, :]).then_inc(d_stf, 1)
                for i in range(2):
                    waits(dve, (d_stf, v * 4 + (2 * r + 1 + i)))
                    dve.bn_aggr(mvf[:, i, :], stf[:, i, :]).then_inc(d_mvf, 1)

            experts(dve, expert)

        @block.gpsimd
        def _(pool):
            pool.memset(ones[:, :], 1.0).then_inc(p_set, 1)
            pool.memset(half[:, :], -0.5).then_inc(p_set, 1)
            pool.memset(epst[:, :], EPS).then_inc(p_set, 1)
            pool.memset(seen[:, :], 0.0).then_inc(p_set, 1)
            pool.memset(vS[:, :, :, :], 0.0).then_inc(p_set, 1)
            pool.memset(onesS[:, :, :], 0.0).then_inc(p_set, 1)
            for k in range(2):
                pool.wait_ge(p_set, 6)
                pool.memset(onesS[:, k, k * HD:(k + 1) * HD], 1.0).then_inc(p_set, 1)
            pool.memset(vh[:, :, :, DK:DK + 1], 1.0).then_inc(p_set, 1)
            pool.memset(empty[:, 0:TOK], 0.0).then_inc(p_set, 1)
            pool.memset(empty[:, TOK:ROW], FAR).then_inc(p_set, 1)
            pool.memset(row[:, :, TOK + 1:ROW], 0.0).then_inc(p_row0, 1)
            pool.wait_ge(p_set, N_SET)

            def normalise(dst, z, mv, ve, rs, s_mv, s_ve, s_rs, s_x, value):
                pool.wait_ge(s_mv, value)
                pool.tensor_tensor(ve[:, :], mv[:, 1:2], epst[0:S, 0:1], ALU.add).then_inc(s_ve, 1)
                pool.wait_ge(s_ve, value)
                pool.tensor_tensor(rs[:, :], ve[:, :], half[0:S, 0:1], ALU.pow).then_inc(s_rs, 1)
                waits(pool, (s_rs, value))
                pool.tensor_scalar(dst, z, mv[:, 0:1], rs[:, 0:1], ALU.subtract, ALU.mult).then_inc(s_x, 1)

            def step(st):
                s = st.s
                for g in range(Q):
                    if g == 0 and st.live(3):
                        if st.live(5):
                            pool.wait_ge(d_z2, st.at(1, 5, 1))
                        normalise(x1[:, st.par(3), :], z1[:, :], mv1, ve1, rs1, d_mv1, p_ve1, p_rs1, p_x1, st.at(1, 3, 1))
                    if g == 2 and st.live(5):
                        if st.live(7):
                            pool.wait_ge(e_row, st.at(1, 7, 1))
                        normalise(x2[:, st.par(5), :], z2[:, :], mv2, ve2, rs2, d_mv2, p_ve2, p_rs2, p_x2, st.at(1, 5, 1))
                    if g == 3 and st.live(6):
                        if st.live(8):
                            pool.wait_ge(o_x3[s], st.half_at(8))
                        normalise(x3[:, s, :], x2[:, s, :], mv3, ve3, rs3, d_mv3, p_ve3, p_rs3, p_x3, st.at(1, 6, 1))
                    if st.live(0):
                        pool.wait_ge(d_max, st.at(Q, 0, g + 1))
                        quad = sc[:, g * HQ:(g + 1) * HQ, :]
                        pool.tensor_tensor(quad, quad,
                                           mx[:, g * HQ:(g + 1) * HQ].rearrange("p (h o) -> p h o", o=1).broadcast_to([S, HQ, S]),
                                           ALU.subtract).then_inc(p_sub, 1)
                    if g == (3 if s == 0 else 1) and st.pair_live(4):
                        waits(pool, (d_row, st.pair(4, 2, 2)), (d_slot, st.pair(4)), (o_empty, 16), (p_row0, 1))
                        pool.indirect_dma_start(slots, bass.IndirectOffsetOnAxis(ap=slot[:, s:s + 1].bitcast(U32), axis=0),
                                                row[:, s, :], None, bounds_check=E * CAP - 1,
                                                oob_is_err=False).then_inc(o_row[s], 16)

            turns(pool, step)

            out_v = out.rearrange("b s d -> (b s) d")
            for i in range(2):
                pool.wait_ge(o_x3[i], 16 * (B // 2))

            def expert(v, r, old1, old2, last):
                m = v * 4 + 2 * r
                n = v * 2 + (r + 1)
                pool.wait_ge(d_mvf, m + 2)
                pool.tensor_tensor(vef[:, :].rearrange("p (i o) -> p i o", o=1), mvf[:, :, 1:2],
                                   epst[0:HALF, 0:2].rearrange("p (i o) -> p i o", o=1), ALU.add).then_inc(p_vef, 1)
                pool.wait_ge(p_vef, n)
                pool.tensor_tensor(rsf[:, :], vef[:, :], half[0:HALF, 0:2], ALU.pow).then_inc(p_rsf, 1)
                for i in range(2):
                    waits(pool, (p_rsf, n), *[(o_yo[r][i], v * 16)] * old2)
                    pool.tensor_scalar(yo[:, r, i, :], zf[:, i, :], mvf[:, i, 0:1], rsf[:, i:i + 1],
                                       ALU.subtract, ALU.mult).then_inc(p_yo, 1)
                pool.wait_ge(d_tok, n)
                for i in range(2):
                    waits(pool, (p_yo, m + (1 + i)))
                    pool.indirect_dma_start(out_v, bass.IndirectOffsetOnAxis(ap=toki[:, r, i:i + 1].bitcast(U32), axis=0),
                                            yo[:, r, i, :], None, bounds_check=T - 1,
                                            oob_is_err=False).then_inc(o_yo[r][i], 16)

            experts(pool, expert)


def layout(x, ctx_1024, mask_1xSxS2_ik1, L0_attn_W_q, L0_attn_W_k, L0_attn_W_v, L0_attn_W_o, L0_attn_W_down_kv,
           L0_attn_W_up_k, L0_attn_W_up_v, L0_xattn_Wq, L0_xattn_bq, L0_xattn_Wk, L0_xattn_bk, L0_xattn_Wv,
           L0_xattn_bv, L0_xattn_Wo, L0_xattn_bo, L0_ffn_Wg, L0_ffn_bg, L0_ffn_W1, L0_ffn_b1, L0_ffn_W2, L0_ffn_b2):
    r = {
        "x": x, "xT": x.transpose(2, 0, 1).reshape(D, T), "ctxT": ctx_1024.transpose(2, 0, 1).reshape(D, B * M),
        "mask": mask_1xSxS2_ik1[0], "wq": L0_attn_W_q, "wkT": L0_attn_W_k.T, "wvT": L0_attn_W_v.T,
        "wo": L0_attn_W_o.reshape(DC, 2, HQ, HD, D).transpose(0, 2, 1, 3, 4).reshape(D, D), "wd": L0_attn_W_down_kv, "wuk": L0_attn_W_up_k, "wuv": L0_attn_W_up_v,
        "xwqT": L0_xattn_Wq.T, "xbq": L0_xattn_bq[:, None], "xwkT": L0_xattn_Wk.T, "xbk": L0_xattn_bk[:, None],
        "xwvT": L0_xattn_Wv.T, "xbv": L0_xattn_bv[:, None], "xwoT": L0_xattn_Wo.T, "xbo": L0_xattn_bo[None, :],
        "wg": L0_ffn_Wg, "bg": L0_ffn_bg[None, :], "w1": L0_ffn_W1,
        "b1": L0_ffn_b1.reshape(E, HC, P).transpose(0, 2, 1), "w2": L0_ffn_W2, "b2": L0_ffn_b2,
        "cst": constants(),
    }
    return {k: np.ascontiguousarray(v) for k, v in r.items()}


def kernel(**inputs):
    import concourse.bacc as bacc
    from concourse.bass_utils import run_bass_kernel_spmd

    arrays = layout(**{k: np.asarray(v) for k, v in inputs.items()})
    nc = bacc.Bacc("TRN2", target_bir_lowering=False, num_devices=1)
    aps = {k: nc.dram_tensor(f"in_{k}", v.shape, mybir.dt.from_np(v.dtype), kind="ExternalInput").ap()
           for k, v in arrays.items()}
    out = nc.dram_tensor("out_0", (B, S, D), F32, kind="ExternalOutput").ap()
    decoder_kernel(nc, aps, out)
    r = run_bass_kernel_spmd(nc, [{f"in_{k}": v for k, v in arrays.items()}], core_ids=[0])
    return r.results[0]["out_0"]
```

```python
from contextlib import ExitStack

import numpy as np

import concourse.bass as bass
from concourse import mybir

F32 = mybir.dt.float32
F32R = mybir.dt.float32r
I32 = mybir.dt.int32
U32 = mybir.dt.uint32
ALU = mybir.AluOpType
ACT = mybir.ActivationFunctionType
AX_X = mybir.AxisListType.X

P = 128
B, S, D = 32, 100, 256
DC = D // P
H, HD = 16, 16
HQ = 4
HP = P // HD
Q = H // HQ
STRIP = P // HQ
DL = 64
M = 361
MT = [(0, 128), (128, 128), (256, 105)]
DK = 64
E, HID = 16, 1024
HC = HID // P
T = B * S
CAP = -(-T // E)
HALF = CAP // 2
ROW = 260
GATE, TOK = D, D + 1
FAR = 1.0e6
MASKED = -1.0e30
EPS = 1e-5
LOOP0, LOOP1 = 4, 14
STEPS = 20

C_ID, C_DEC, C_TRI, C_REV, C_TOK = 0, 128, 228, 328, 360
C_ALL = 392


def constants():
    c = np.zeros((P, C_ALL), np.float32)
    i = np.arange(S)
    c[:, C_ID:C_ID + P] = np.eye(P)
    t = i.astype(np.float32)
    c[:S, C_DEC:C_DEC + S] = np.exp(np.float32(-0.01) * np.abs(t[:, None] - t[None, :])) / np.float32(16.0)
    c[:S, C_TRI:C_TRI + S] = i[:, None] <= i[None, :]
    c[:, C_REV:C_REV + 2 * E] = np.tile(E - np.arange(E), 2)[None, :]
    c[:S, C_TOK:C_TOK + B] = i[:, None] + S * np.arange(B)[None, :]
    return c


def decoder_kernel(nc, a, out):
    ctx = ExitStack()
    with ctx:
        def sb(name, shape, dt=F32):
            return ctx.enter_context(nc.sbuf_tensor(name, shape, dt))

        def sem(name):
            return ctx.enter_context(nc.semaphore(name))

        bank = [ctx.enter_context(nc.psum_tensor(f"bank{i}", [P, 512], F32)) for i in range(8)]
        psS, psT, psO, M0, M1, M2 = bank[0:2], bank[2:4], bank[4], bank[5], bank[6], bank[7]
        psH, psX, psY = bank[0:4], bank[4], bank[5:7]

        cst = sb("cst", [P, C_ALL])
        ident = cst[:, C_ID:C_ID + P]
        dec = cst[0:S, C_DEC:C_DEC + S]
        tri = cst[0:S, C_TRI:C_TRI + S]
        rev = cst[0:S, C_REV:C_REV + 2 * E].rearrange("p (s e) -> p s e", s=2)
        tok = cst[0:S, C_TOK:C_TOK + B]
        ones = sb("ones", [P, P])
        half = sb("half", [P, 2])
        epst = sb("epst", [P, 2])
        wq = sb("wq", [P, DC, D])
        wkT = sb("wkT", [P, DC, D])
        wvT = sb("wvT", [P, DC, D])
        wd = sb("wd", [P, DC, DL])
        wc = sb("wc", [P, DC, DL])
        wuk = sb("wuk", [DL, D])
        wuv = sb("wuv", [DL, D])
        wo = sb("wo", [P, DC, D])
        xwq = sb("xwq", [P, DC, DK])
        xwkv = sb("xwkv", [P, DC, 2 * DK])
        xbq = sb("xbq", [DK, 1])
        xbkv = sb("xbkv", [2 * DK, 1])
        xwo = sb("xwo", [DK + 1, D])
        wg = sb("wg", [P, DC, E])
        bg = sb("bg", [S, E])
        mski = sb("mski", [S, M], I32)
        msk = sb("msk", [S, M])
        empty = sb("empty", [P, ROW])

        xT = sb("xT", [P, DC, 2 * S])
        xN = sb("xN", [S, 2, D])
        qh, ql = sb("qh", [P, DC, 2 * S], F32R), sb("ql", [P, DC, 2 * S], F32R)
        latT = sb("latT", [DL, 2 * S])
        khl = sb("khl", [P, DC, 2, S], F32R)
        kh, kl = khl[:, :, 0, :], khl[:, :, 1, :]
        kM = sb("kM", [P, 2, DC, 2, HP, S], F32R)
        vS = sb("vS", [S, 2, H, STRIP])
        onesS = sb("onesS", [S, 2, STRIP])
        space = sb("space", [P, H * S])
        sc = space[0:S, :].rearrange("p (h k) -> p h k", h=H)
        mx = sb("mx", [S, H])
        space2 = sb("space2", [S, H * S])
        pr = space2[:, :].rearrange("p (h k) -> p h k", h=H)
        pT = sb("pT", [S, 2, HQ, S])
        rec = sb("rec", [P, DC * S])
        aT = sb("aT", [P, DC, S])
        z1 = sb("z1", [S, D])
        st1, mv1, ve1, rs1 = sb("st1", [S, 6]), sb("mv1", [S, 2]), sb("ve1", [S, 1]), sb("rs1", [S, 2])
        x1 = sb("x1", [S, 2, D])

        cT = sb("cT", [P, 2, DC, M])
        x1T = sb("x1T", [P, DC, S])
        qhT = sb("qhT", [DK, S])
        kvT = sb("kvT", [2 * DK, M])
        vh = sb("vh", [P, 2, 3, DK + 1])
        sB = sb("sB", [S, M])
        mxB = sb("mxB", [S, 1])
        nmB = sb("nmB", [S, 1])
        pB = sb("pB", [S, M])
        rsB = sb("rsB", [S, 2])
        rvB = sb("rvB", [S, 1])
        pBT = sb("pBT", [P, 3, S])
        oT = sb("oT", [DK + 1, S])
        z2 = sb("z2", [S, D])
        st2, mv2, ve2, rs2 = sb("st2", [S, 6]), sb("mv2", [S, 2]), sb("ve2", [S, 1]), sb("rs2", [S, 2])
        x2 = sb("x2", [S, 2, D])

        x2T = sb("x2T", [P, DC, S])
        lg = sb("lg", [S, 2, E])
        st3, mv3, ve3, rs3 = sb("st3", [S, 6]), sb("mv3", [S, 2]), sb("ve3", [S, 1]), sb("rs3", [S, 2])
        x3 = sb("x3", [S, 2, D])
        row = sb("row", [S, 2, ROW])
        lmax = sb("lmax", [S, 2])
        ld = sb("ld", [S, 2, E])
        le = sb("le", [S, 2, E])
        key = sb("key", [S, 2, E])
        kmax = sb("kmax", [S, 2])
        oh = sb("oh", [S, 2, E])
        seen = sb("seen", [S, E])
        pose = sb("pose", [S, 2, E])
        pos = sb("pos", [S, 2])
        over = sb("over", [S, 2])
        base = sb("base", [S, 2])
        slot = sb("slot", [S, 2], I32)
        den = sb("den", [S, 2])

        w1 = sb("w1", [P, 2, DC, HID])
        w2 = sb("w2", [P, 2, HC, D])
        b1 = sb("b1", [P, 2, HC])
        b2 = sb("b2", [HALF, 2, D])
        bx = space2[:, 0:4 * ROW].rearrange("p (r i c) -> p r i c", r=2, i=2)
        bxT = sb("bxT", [P, 2, DC, CAP])
        bz = sb("bz", [HALF, 2, 2, ROW])
        hT = space[:, :].rearrange("p (j t) -> p j t", j=HC)
        hh, hl = sb("hh", [P, 2, HC, CAP], F32R), sb("hl", [P, 2, HC, CAP], F32R)
        w2h, w2l = sb("w2h", [P, 2, HC, D], F32R), sb("w2l", [P, 2, HC, D], F32R)
        yb = sb("yb", [HALF, 2, D])
        zf = space2[:, 4 * ROW:4 * ROW + 2 * D].rearrange("p (i d) -> p i d", i=2)
        stf, mvf = sb("stf", [HALF, 2, 6]), sb("mvf", [HALF, 2, 2])
        vef, rsf = sb("vef", [HALF, 2]), sb("rsf", [HALF, 2])
        yo = sb("yo", [HALF, 2, 2, D])
        toki = sb("toki", [HALF, 2, 2], I32)

        slots = nc.dram_tensor("slots", [E * CAP, ROW], F32, kind="Internal").ap()

        l_w0, l_w, l_late, l_xT = sem("l_w0"), sem("l_w"), sem("l_late"), sem("l_xT")
        l_xN = [sem(f"l_xN{i}") for i in range(2)]
        l_cT = [sem(f"l_cT{i}") for i in range(2)]
        l_w1 = [sem(f"l_w1{i}") for i in range(2)]
        l_w2 = [sem(f"l_w2{i}") for i in range(2)]
        l_bx = [sem(f"l_bx{i}") for i in range(2)]
        l_bz = [sem(f"l_bz{i}") for i in range(2)]
        s_wc, s_q, s_lat, s_k, s_v, s_S, s_PT, s_PV, s_wo = map(
            sem, "s_wc s_q s_lat s_k s_v s_S s_PT s_PV s_wo".split())
        s_x1T, s_qh, s_kv, s_vh, s_B, s_BT, s_o, s_wo2, s_x2T, s_lg, s_cum = map(
            sem, "s_x1T s_qh s_kv s_vh s_B s_BT s_o s_wo2 s_x2T s_lg s_cum".split())
        s_bT, s_h, s_y = map(sem, "s_bT s_h s_y".split())
        e_q, e_v, e_exp, e_PT, e_x1T, e_qh, e_kv, e_vh, e_BT, e_B, e_o, e_x2T, e_le, e_row, e_x1, e_x2, e_x3 = map(
            sem, "e_q e_v e_exp e_PT e_x1T e_qh e_kv e_vh e_BT e_B e_o e_x2T e_le e_row e_x1 e_x2 e_x3".split())
        e_bT, e_h, e_hh, e_w2 = map(sem, "e_bT e_h e_hh e_w2".split())
        d_msk, d_wc, d_lat, d_max, d_rec, d_aT, d_z1, d_st1, d_mv1 = map(
            sem, "d_msk d_wc d_lat d_max d_rec d_aT d_z1 d_st1 d_mv1".split())
        d_B, d_nm, d_rv, d_z2, d_st2, d_mv2, d_lg, d_st3, d_mv3 = map(
            sem, "d_B d_nm d_rv d_z2 d_st2 d_mv2 d_lg d_st3 d_mv3".split())
        d_lmax, d_ld, d_key, d_kmax, d_oh, d_pose, d_pos, d_base, d_slot, d_seen, d_den, d_row = map(
            sem, "d_lmax d_ld d_key d_kmax d_oh d_pose d_pos d_base d_slot d_seen d_den d_row".split())
        d_hl, d_w2 = sem("d_hl"), sem("d_w2")
        d_zero, d_kh, d_kl, d_ql = map(sem, "d_zero d_kh d_kl d_ql".split())
        l_k = [sem(f"l_k{i}") for i in range(2)]
        d_h, d_yb, d_zf, d_stf, d_mvf, d_tok = map(sem, "d_h d_yb d_zf d_stf d_mvf d_tok".split())
        p_sub, p_zero, p_row0, p_set, p_ve1, p_rs1, p_sh1, p_ve2, p_rs2, p_sh2, p_ve3, p_rs3, p_sh3 = map(
            sem, "p_sub p_zero p_row0 p_set p_ve1 p_rs1 p_sh1 p_ve2 p_rs2 p_sh2 p_ve3 p_rs3 p_sh3".split())
        p_vef, p_rsf, p_yo = map(sem, "p_vef p_rsf p_yo".split())
        o_empty = sem("o_empty")
        o_x3 = [sem(f"o_x3{i}") for i in range(2)]
        o_row = [sem(f"o_row{i}") for i in range(2)]
        o_yo = [[sem(f"o_yo{i}{j}") for j in range(2)] for i in range(2)]

        class Step:

            def __init__(self, u, s):
                self.u, self.s = u, s
                self.peeled = isinstance(u, int)

            def live(self, k):
                return not self.peeled or 0 <= 2 * self.u + self.s - k < B

            def at(self, per, k, j):
                return self.u * (2 * per) + (per * (self.s - k) + j)

            def half_at(self, k):
                return self.u * 16 + (((self.s - k) // 2) + 1) * 16

            def par(self, k):
                return (self.s - k) % 2

            def pair_live(self, k):
                return not self.peeled or 0 <= self.u - k < B // 2

            def pair(self, k, per=1, j=1):
                return self.u * per + (j - k * per)

            def batch(self, k):
                return self.u * 2 + (self.s - k)

        def experts(eng, expert):
            for r in range(2):
                expert(0, r, r == 1, False, False)
            with eng.Fori(1, E // 2 - 1) as v:
                for r in range(2):
                    expert(v, r, True, True, False)
            for r in range(2):
                expert(E // 2 - 1, r, True, True, r == 1)

        def turns(eng, step):
            for u in range(LOOP0):
                for s in range(2):
                    step(Step(u, s))
            with eng.Fori(LOOP0, LOOP1) as u:
                for s in range(2):
                    step(Step(u, s))
            for u in range(LOOP1, STEPS):
                for s in range(2):
                    step(Step(u, s))

        N_W = 3
        N_LATE = 13
        N_SET = 11

        def waits(eng, *pairs):
            values = [v if isinstance(v, int) else eng.to_reg(v) for _, v in pairs]
            eng.wait_ge(l_w, 16 * N_W)
            for (s_, _), v in zip(pairs, values):
                eng.wait_ge(s_, v)

        block = ctx.enter_context(nc.Block())

        @block.sync
        def _(sp):
            ctx_v = a["ctxT"].rearrange("(c p) (b m) -> p c b m", p=P, m=M)
            xT_v = a["xT"].rearrange("(c p) t -> p c t", p=P)
            out_v = out.rearrange("b s d -> (b s) d")

            def load_xT(t0):
                sp.dma_start(xT[:, :, :], xT_v[:, :, bass.ds(t0, 2 * S)]).then_inc(l_xT, 16)

            def load_xN(b, i):
                sp.dma_start(xN[:, i, :], a["x"][bass.ds(b, 1), :, :].rearrange("o s d -> (o s) d")).then_inc(l_xN[i], 16)

            def load_cT(b, i):
                sp.dma_start(cT[:, i, :, :], ctx_v[:, :, bass.ds(b, 1), :].rearrange("p c o m -> p c (o m)")).then_inc(l_cT[i], 16)

            def load_w1(e, r):
                sp.dma_start(w1[:, r, :, :], a["w1"][bass.ds(e, 1), :, :].rearrange("o (c p) h -> p (o c) h", p=P)).then_inc(l_w1[r], 16)

            def load_w2(e, r):
                sp.dma_start(w2[:, r, :, :], a["w2"][bass.ds(e, 1), :, :].rearrange("o (c p) h -> p (o c) h", p=P)).then_inc(l_w2[r], 16)

            def load_b1(e, r):
                sp.dma_start(b1[:, r, :], a["b1"][bass.ds(e, 1), :, :].rearrange("o p j -> p (o j)")).then_inc(l_w1[r], 16)

            def load_b2(e, r):
                sp.dma_start(b2[:, r, :], a["b2"][bass.ds(e, 1), :].broadcast_to([HALF, D])).then_inc(l_bz[r], 16)

            def load_bx(e, r):
                sp.dma_start(bx[:, r, :, :], slots[bass.ds(e * CAP, CAP), :].rearrange("(i p) c -> p i c", p=HALF)).then_inc(l_bx[r], 16)

            def load_bz(e, r):
                sp.dma_start(bz[:, r, :, :], slots[bass.ds(e * CAP, CAP), :].rearrange("(i p) c -> p i c", p=HALF)).then_inc(l_bz[r], 16)

            def lay_out_keys(st, k):
                waits(sp, (d_kl, st.at(1, k, 1)), *[(s_S, st.at(Q, k + 2, Q))] * st.live(k + 2))
                for h in range(HP):
                    rows = slice(h * HD, (h + 1) * HD)
                    sp.dma_start(kM[rows, st.par(k), :, :, h, :].bitcast(F32), khl[rows, :, :, :].bitcast(F32)).then_inc(l_k[h // HQ], 16)

            n, sem_w = [0], [l_w]

            def w(dst, src):
                sp.dma_start(dst, src).then_inc(sem_w[0], 16)
                n[0] += 1

            for tile, name in ((wd, "wd"), (wkT, "wkT"), (wvT, "wvT")):
                sp.dma_start(tile[:, :, :], a[name].rearrange("(c p) n -> p c n", p=P)).then_inc(l_w0, 16)
            load_xT(0)
            w(cst[:, :], a["cst"])
            w(wq[:, :, :], a["wq"].rearrange("(c p) n -> p c n", p=P))
            w(wuk[:, :], a["wuk"])
            assert n[0] == N_W, n[0]
            sem_w[0] = l_late
            w(wuv[:, :], a["wuv"])
            w(mski[:, :], a["mask"])
            load_xN(0, 0)
            load_xN(1, 1)
            w(wo[:, :, :], a["wo"].rearrange("(c p) n -> p c n", p=P))
            w(xwq[:, :, :], a["xwqT"].rearrange("(c p) n -> p c n", p=P))
            w(xwkv[:, :, 0:DK], a["xwkT"].rearrange("(c p) n -> p c n", p=P))
            w(xwkv[:, :, DK:2 * DK], a["xwvT"].rearrange("(c p) n -> p c n", p=P))
            w(xbq[:, :], a["xbq"])
            w(xbkv[0:DK, :], a["xbk"])
            w(xbkv[DK:2 * DK, :], a["xbv"])
            w(xwo[0:DK, :], a["xwoT"])
            w(xwo[DK:DK + 1, :], a["xbo"])
            w(wg[:, :, :], a["wg"].rearrange("(c p) n -> p c n", p=P))
            w(bg[:, :], a["bg"].broadcast_to([S, E]))
            sp.wait_ge(d_zero, 1)
            lay_out_keys(Step(0, 0), 0)
            load_cT(0, 0)
            load_cT(1, 1)
            sp.wait_ge(s_q, 1)
            load_xT(2 * S)
            assert n[0] == N_W + N_LATE, n[0]

            def step(st):
                s = st.s
                if st.live(7):
                    sp.wait_ge(e_x3, st.at(1, 7, 1))
                    sp.dma_start(out_v[bass.ds(st.batch(7) * S, S), :], x3[:, st.par(7), :]).then_inc(o_x3[st.par(7)], 16)
                if st.live(3) and st.live(1):
                    sp.wait_ge(s_kv, st.at(1, 3, 1))
                    load_cT(st.batch(1), st.par(1))
                if st.live(2) and st.live(0):
                    sp.wait_ge(d_z1, st.at(1, 2, 1))
                    load_xN(st.batch(0), s)
                if st.live(-1):
                    if st.peeled and st.u == 0 and s == 0:
                        sp.wait_ge(p_zero, 1)
                    lay_out_keys(st, -1)
                if st.peeled and st.u == 1 and s == 0:
                    sp.wait_ge(p_set, N_SET)
                    sp.dma_start(slots.rearrange("(n p) c -> p n c", p=P),
                                 empty[:, :].rearrange("p (o c) -> p o c", o=1).broadcast_to([P, E * CAP // P, ROW])).then_inc(o_empty, 16)
                if st.peeled and st.u in (2, 3) and s == 0:
                    r = st.u - 2
                    load_w1(r, r)
                    load_b1(r, r)
                    load_w2(r, r)
                    load_b2(r, r)
                if s == 1 and st.pair_live(-2):
                    sp.wait_ge(s_q, st.pair(-1))
                    load_xT(st.batch(-3) * S)

            turns(sp, step)
            for i in range(2):
                sp.wait_ge(o_row[i], 16 * (B // 2))
            for r in range(2):
                load_bx(r, r)
                load_bz(r, r)

            def residual_rows(v, r):
                waits(sp, (d_zf, v * 4 + 2 * r), (d_tok, v * 2 + r))
                load_b2(v * 2 + (r + 1), 1 - r)
                load_bz(v * 2 + (r + 1), 1 - r)

            def follow(v, r, later):
                n1 = v * 2 + (r + 1)
                waits(sp, (s_bT, n1))
                load_bx(v * 2 + (2 + r), r)
                if later:
                    residual_rows(v, r)
                waits(sp, (s_h, v * 8 + (4 * r + 4)), (e_h, v * 4 + (2 * r + 2)), (d_h, v * 4 + (2 * r + 2)))
                load_w1(v * 2 + (2 + r), r)
                load_b1(v * 2 + (2 + r), r)
                waits(sp, (d_w2, n1))
                load_w2(v * 2 + (2 + r), r)

            for r in range(2):
                follow(0, r, r == 1)
            with sp.Fori(1, E // 2 - 1) as v:
                for r in range(2):
                    follow(v, r, True)
            residual_rows(E // 2 - 1, 0)
            for r in range(2):
                for i in range(2):
                    sp.wait_ge(o_yo[r][i], 16 * (E // 2))
                sp.wait_ge(o_x3[r], 16 * (B // 2))

        @block.tensor
        def _(pe):
            mm = pe.matmul

            def wait_latest(*users):
                for there, s_, value in users:
                    if there:
                        pe.wait_ge(s_, value)
                        return

            pe.wait_ge(l_w0, 16 * 3)
            for c in range(DC):
                for w_, first in ((wkT, True), (wvT, False)):
                    for k in range(DC):
                        last = mm(M0[:, c * DL:(c + 1) * DL], w_[:, k, c * P:(c + 1) * P], wd[:, k, :],
                                  start=first and k == 0, stop=not first and k == DC - 1)
            last.then_inc(s_wc, 1)
            pe.wait_ge(d_wc, 1)
            pe.wait_ge(p_set, N_SET)

            def project_latent(p):
                pe.wait_ge(l_xT, p * 16)
                for c in range(DC):
                    i = mm(M1[0:DL, 0:2 * S], wc[:, c, :], xT[:, c, :], start=c == 0, stop=c == DC - 1)
                i.then_inc(s_lat, 1)

            def project_q():
                for o in range(DC):
                    for c in range(DC):
                        i = mm(M2[:, o * 2 * S:(o + 1) * 2 * S], wq[:, c, o * P:(o + 1) * P], xT[:, c, :],
                               start=c == 0, stop=c == DC - 1)
                i.then_inc(s_q, 1)

            def project_k(half_):
                for o in range(DC):
                    i = mm(M0[:, o * S:(o + 1) * S], wuk[:, o * P:(o + 1) * P], latT[:, half_ * S:(half_ + 1) * S],
                           start=True, stop=True)
                i.then_inc(s_k, 1)

            def context_values(st, *bank_free):
                waits(pe, *bank_free)
                for m, (m0, mn) in enumerate(MT):
                    i = pe.transpose(M1[0:mn, m * DK:(m + 1) * DK], kvT[DK:2 * DK, m0:m0 + mn],
                                     ident[DK:2 * DK, DK:2 * DK])
                i.then_inc(s_vh, 1)

            project_latent(1)
            pe.wait_ge(l_w, 16 * N_W)
            pe.wait_ge(d_lat, 1)
            project_k(0)
            project_q()

            def project_v(half_, bank_):
                mm(bank_[0:S, 0:D], latT[:, half_ * S:(half_ + 1) * S], wuv[:, :], start=True, stop=True).then_inc(s_v, 1)

            def project_cross(st, k):
                pe.wait_ge(e_o, st.at(1, k, 1))
                mm(M1[0:S, 0:D], oT[:, :], xwo[:, :], start=True, stop=True).then_inc(s_wo2, 1)

            def cross_scores(st):
                pe.wait_ge(e_qh, st.at(1, 4, 1))
                mm(M0[0:S, 0:M], qhT[:, :], kvT[0:DK, :], start=True, stop=True).then_inc(s_B, 1)

            def after_scores0(st):
                s = st.s
                if st.live(3):
                    pe.wait_ge(l_cT[st.par(3)], st.half_at(3))
                    wait_latest((st.live(5), d_z2, st.at(1, 5, 1)),
                                (s == 0 and st.live(4), e_vh, st.at(1, 4, 1)), (s == 0 and st.pair_live(0), d_lat, st.pair(0)),
                                (st.live(1), e_v, st.at(1, 1, 1)))
                    for c in range(DC):
                        i = mm(M1[:, 0:M], xwkv[:, c, :], cT[:, st.par(3), c, :], start=c == 0, stop=c == DC - 1)
                    i.then_inc(s_kv, 1)

            def after_scores1(st):
                s = st.s
                if st.live(2):
                    pe.wait_ge(d_aT, st.at(1, 2, 1))
                    wait_latest((st.live(4), d_B, st.at(1, 4, 1)), (st.live(0), d_kl, st.at(1, 0, 1)), (st.live(3), d_z1, st.at(1, 3, 1)))
                    for c in range(DC):
                        i = mm(M0[0:S, 0:D], aT[:, c, :], wo[:, c, :], start=c == 0, stop=c == DC - 1)
                    i.then_inc(s_wo, 1)
                if st.live(6):
                    pe.wait_ge(e_x2, st.at(1, 6, 1))
                    wait_latest((s == 1 and st.live(0), e_v, st.at(1, 0, 1)), (s == 0 and st.pair_live(0), d_ql, st.pair(0)),
                                (st.live(5), e_BT, st.at(1, 5, 1)), (s == 1 and st.pair_live(4), d_pose, st.pair(4)),
                                (st.live(7), d_lg, st.at(1, 7, 1)))
                    for c in range(DC):
                        i = pe.transpose(M2[:, c * S:(c + 1) * S], x2[:, st.par(6), c * P:(c + 1) * P], ident[0:S, 0:S])
                    i.then_inc(s_x2T, 1)
                if st.live(3):
                    pe.wait_ge(e_x1, st.at(1, 3, 1))
                    pe.wait_ge(e_kv, st.at(1, 3, 1))
                    if s == 1 and st.pair_live(-1):
                        pe.wait_ge(d_lat, st.pair(-1))
                    for c in range(DC):
                        i = pe.transpose(M1[:, c * S:(c + 1) * S], x1[:, st.par(3), c * P:(c + 1) * P], ident[0:S, 0:S])
                    i.then_inc(s_x1T, 1)

            def after_scores2(st):
                s = st.s
                if st.live(3):
                    context_values(st, (e_x1T, st.at(1, 3, 1)))
                if s == 0 and st.pair_live(4):
                    pe.wait_ge(d_oh, st.pair(4))
                    wait_latest((st.live(6), e_x2T, st.at(1, 6, 1)), (st.pair_live(0), d_ql, st.pair(0)), (st.live(5), e_BT, st.at(1, 5, 1)),
                                (st.live(7), d_lg, st.at(1, 7, 1)), (st.pair_live(5), d_pose, st.pair(5)))
                    places = M2[0:S, E:3 * E]
                    mm(places, tri, oh[:, :, :], start=True, stop=False)
                    mm(places, ones[0:S, 0:S],
                       seen[:, :].rearrange("p (o e) -> p o e", o=1).broadcast_to([S, 2, E]), start=False, stop=False)
                    mm(M2[0:S, 2 * E:3 * E], ones[0:S, 0:S], oh[:, 0, :], start=False, stop=True).then_inc(s_cum, 1)
                if st.live(6):
                    pe.wait_ge(e_x2T, st.at(1, 6, 1))
                    for c in range(DC):
                        i = mm(M2[0:S, 0:E], x2T[:, c, :], wg[:, c, :], start=c == 0, stop=c == DC - 1)
                    i.then_inc(s_lg, 1)
                if st.live(3):
                    pe.wait_ge(e_x1T, st.at(1, 3, 1))
                    if st.live(-1):
                        pe.wait_ge(d_kl, st.at(1, -1, 1))
                    wait_latest((st.live(2), d_z1, st.at(1, 2, 1)), (True, d_B, st.at(1, 4, 1)))
                    for c in range(DC):
                        i = mm(M0[0:DK, 0:S], xwq[:, c, :], x1T[:, c, :], start=c == 0, stop=c == DC - 1)
                    i.then_inc(s_qh, 1)

            def next_latents(st):
                wait_latest((st.live(3), e_kv, st.at(1, 3, 1)), (st.live(1), e_v, st.at(1, 1, 1)))
                project_latent(st.pair(-1))

            def next_keys(st):
                if st.s == 1:
                    pe.wait_ge(d_lat, st.pair(-1))
                wait_latest((st.live(2), d_z1, st.at(1, 2, 1)), (st.live(4), d_B, st.at(1, 4, 1)),
                            (True, d_kl, st.at(1, 0, 1)))
                project_k(1 - st.s)

            def before_last_scores(st):
                s = st.s
                if s == 0 and st.live(0):
                    if st.peeled and st.u == 0:
                        pe.wait_ge(l_late, 16 * N_LATE)
                    wait_latest((st.live(3), e_vh, st.at(1, 3, 1)), (True, d_lat, st.pair(0)))
                    project_v(0, M1)
                if st.live(4):
                    pe.wait_ge(e_B, st.at(1, 4, 1))
                    wait_latest((s == 0 and st.pair_live(4), d_pose, st.pair(4)), (st.live(6), d_lg, st.at(1, 6, 1)),
                                (s == 1 and st.live(0), e_v, st.at(1, 0, 1)), (s == 0 and st.pair_live(0), d_ql, st.pair(0)),
                                (st.live(5), e_BT, st.at(1, 5, 1)))
                    for m, (m0, mn) in enumerate(MT):
                        i = pe.transpose(M2[0:mn, m * S:(m + 1) * S], pB[:, m0:m0 + mn], ident[0:S, 0:S])
                    i.then_inc(s_BT, 1)

            def ends(st):
                s = st.s
                if st.live(4):
                    pe.wait_ge(e_BT, st.at(1, 4, 1))
                if st.live(4):
                    wait_latest((s == 0 and st.live(0), e_v, st.at(1, 0, 1)),
                                (st.live(3), e_vh, st.at(1, 3, 1)), (s == 0 and st.live(5), d_z2, st.at(1, 5, 1)),
                                (st.live(5), e_o, st.at(1, 5, 1)))
                    for m, (m0, mn) in enumerate(MT):
                        i = mm(M1[0:DK + 1, 0:S], vh[0:mn, st.par(4), m, :], pBT[0:mn, m, :], start=m == 0, stop=m == 2)
                    i.then_inc(s_o, 1)
                if s == 1 and st.pair_live(-1):
                    if not st.live(4):
                        pe.wait_ge(e_v, st.at(1, 0, 1))
                    project_q()
                if s == 1 and st.live(4):
                    project_cross(st, 4)
                if s == 0 and st.live(-1):
                    if not st.live(4):
                        pe.wait_ge(d_ql, st.pair(0))
                    project_v(1, M2)

            def step(st):
                s = st.s
                for g in range(Q):
                    if st.live(1):
                        pe.wait_ge(e_exp, st.at(Q, 1, g + 1))
                        if g >= 2 or st.live(2):
                            pe.wait_ge(e_PT, st.at(Q, 1, g - 1))
                        for j in range(HQ):
                            i = pe.transpose(psT[g % 2][0:S, j * S:(j + 1) * S], pr[:, g * HQ + j, :], ident[0:S, 0:S])
                        i.then_inc(s_PT, 1)
                    if g == 0 and s == 0 and st.live(4):
                        cross_scores(st)
                    if g == 0 and s == 1 and st.live(5):
                        project_cross(st, 5)
                    if g == 1 and s == 1 and st.pair_live(-1):
                        next_latents(st)
                    if g == 2 and st.live(-1):
                        next_keys(st)
                    if g == 3:
                        before_last_scores(st)
                    if st.live(0):
                        if g == 0:
                            if s == 0:
                                pe.wait_ge(d_ql, st.pair(0))
                        if g < 2:
                            pe.wait_ge(l_k[g], st.at(16 * HQ, 0, 16 * HQ))
                        if g >= 2 or st.live(1):
                            pe.wait_ge(d_max, st.at(Q, 0, g - 1))
                        c, h0 = g // 2, HQ * (g % 2)
                        for q_, k_, first, end in ((qh, 0, True, False), (ql, 0, False, False), (qh, 1, False, True)):
                            i = mm(psS[g % 2][0:S, 0:HQ * S], q_[:, c, s * S:(s + 1) * S], kM[:, s, c, k_, h0:h0 + HQ, :],
                                   start=first, stop=end)
                        i.then_inc(s_S, 1)
                    if g == 0 and s == 1 and st.live(4):
                        cross_scores(st)
                    if g < 3:
                        (after_scores0, after_scores1, after_scores2)[g](st)
                    if st.live(1):
                        pe.wait_ge(e_PT, st.at(Q, 1, g + 1))
                        if g == 0:
                            pe.wait_ge(e_v, st.at(1, 1, 1))
                            if st.live(2):
                                pe.wait_ge(d_aT, st.at(1, 2, 1))
                        for k in range(2):
                            for j in range(HQ):
                                rows = slice(j * STRIP, (j + 1) * STRIP)
                                cols = slice((k * DC + g // 2) * S, (k * DC + g // 2 + 1) * S)
                                of = vS[:, st.par(1), g * HQ + j, :] if k == 0 else onesS[:, g % 2, :]
                                i = mm(psO[rows, cols], of, pT[:, g % 2, j, :], start=g == k == 0, stop=g == Q - 1 and k == 1,
                                       tile_position=(0, j * STRIP))
                        i.then_inc(s_PV, 1)
                ends(st)

            turns(pe, step)

            for s_, n in ((d_z2, B), (d_max, Q * B), (e_PT, Q * B), (d_aT, B), (d_pose, B // 2), (d_B, B), (e_o, B)):
                pe.wait_ge(s_, n)

            def rows_in(r, loaded):
                pe.wait_ge(l_bx[r], loaded)
                for c in range(DC):
                    for i in range(2):
                        k = c * 2 + i
                        ins = pe.transpose(psX[:, k * HALF:(k + 1) * HALF], bx[:, r, i, c * P:(c + 1) * P], ident[0:HALF, 0:HALF])
                ins.then_inc(s_bT, 1)

            rows_in(0, 16)

            def expert(v, r, old1, old2, last):
                n2 = v * 4 + 2 * r
                pe.wait_ge(e_bT, v * 2 + (r + 1))
                pe.wait_ge(l_w1[r], v * 32 + 32)
                for q in range(HC // 2):
                    if old1:
                        pe.wait_ge(e_h if q % 2 == 0 else d_h, n2 + (q // 2 - 1))
                    for j in (2 * q, 2 * q + 1):
                        for c in range(DC):
                            i = mm(psH[q][:, (j % 2) * CAP:(j % 2 + 1) * CAP], w1[:, r, c, j * P:(j + 1) * P],
                                   bxT[:, r, c, :], start=c == 0, stop=c == DC - 1)
                    i.then_inc(s_h, 1)
                if not last:
                    rows_in(1 - r, v * 16 + (16 if r == 0 else 32))
                if old1:
                    second_layer(v, r)

            def second_layer(v, r):
                n = v * 2 + r
                pe.wait_ge(e_hh, v * 8 + 4 * r)
                pe.wait_ge(d_hl, v * 8 + 4 * r)
                pe.wait_ge(e_w2, n)
                pe.wait_ge(d_w2, n)
                if not isinstance(v, int) or v * 2 + r > 2:
                    pe.wait_ge(d_yb, v * 2 + (r - 2))
                k = 1 - r
                for i in range(2):
                    rows = slice(i * HALF, (i + 1) * HALF)
                    for j in range(HC):
                        for h_, w_, first, end in ((hh, w2h, True, False), (hh, w2l, False, False), (hl, w2h, False, True)):
                            ins = mm(psY[k][0:HALF, i * D:(i + 1) * D], h_[:, k, j, rows], w_[:, k, j, :],
                                     start=j == 0 and first, stop=j == HC - 1 and end)
                ins.then_inc(s_y, 1)

            experts(pe, expert)
            second_layer(E // 2, 0)

        @block.scalar
        def _(act):
            def copy(dst, src):
                return act.activation(dst, src, ACT.Copy)

            def put_q(p):
                act.wait_ge(s_q, p)
                copy(qh[:, :, :].rearrange("p c t -> p (c t)"), M2[:, 0:DC * 2 * S]).then_inc(e_q, 1)

            def put_v(st, k, bank_):
                act.wait_ge(s_v, st.at(1, k, 1))
                for o in range(2):
                    i = copy(vS[:, st.par(k), :, :].rearrange("p (c o j) w -> p c o j w", c=DC, o=2)[:, :, o, :, o * HD:(o + 1) * HD],
                             bank_[0:S, 0:D].rearrange("p (c o j d) -> p c o j d", c=DC, o=2, j=HQ)[:, :, o, :, :])
                i.then_inc(e_v, 1)

            def normalise(dst, z, rs, s_sh, s_x, value, *free):
                waits(act, (s_sh, value), *free)
                act.activation(dst, z, ACT.Identity, bias=rs[:, 1:2], scale=rs[:, 0:1]).then_inc(s_x, 1)

            def put_context_values(st):
                act.wait_ge(s_vh, st.at(1, 3, 1))
                copy(vh[:, st.par(3), 0:2, 0:DK], M1[:, 0:2 * DK].rearrange("p (m d) -> p m d", m=2))
                copy(vh[0:MT[2][1], st.par(3), 2, 0:DK], M1[0:MT[2][1], 2 * DK:3 * DK]).then_inc(e_vh, 1)

            def probabilities(st, k, g):
                act.wait_ge(p_sub, st.at(Q, k, g + 1))
                if st.live(k + 1):
                    act.wait_ge(s_PT, st.at(Q, k + 1, g + 1))
                act.activation(pr[:, g * HQ:(g + 1) * HQ, :], sc[:, g * HQ:(g + 1) * HQ, :], ACT.Exp).then_inc(e_exp, 1)

            put_q(1)

            def step(st):
                s = st.s
                for g in range(Q):
                    if st.live(1):
                        act.wait_ge(s_PT, st.at(Q, 1, g + 1))
                        if g >= 2 or st.live(2):
                            act.wait_ge(s_PV, st.at(Q, 1, g - 1))
                        copy(pT[:, g % 2, :, :].rearrange("p h q -> p (h q)"), psT[g % 2][0:S, 0:HQ * S]).then_inc(e_PT, 1)
                    if g == 0:
                        if st.live(3):
                            act.wait_ge(s_kv, st.at(1, 3, 1))
                            if st.live(4):
                                act.wait_ge(s_B, st.at(1, 4, 1))
                            act.activation(kvT[:, :], M1[:, 0:M], ACT.Identity, bias=xbkv[:, :]).then_inc(e_kv, 1)
                        if st.live(3):
                            normalise(x1[:, st.par(3), :], z1[:, :], rs1, p_sh1, e_x1, st.at(1, 3, 1), *[(d_z2, st.at(1, 5, 1))] * st.live(5))
                        if st.live(1):
                            probabilities(st, 1, Q - 1)
                        if st.live(7):
                            normalise(x3[:, st.par(7), :], x2[:, st.par(7), :], rs3, p_sh3, e_x3, st.at(1, 7, 1),
                                      *[(o_x3[st.par(7)], st.half_at(9))] * st.live(9))
                    if g == 1:
                        if s == 0 and st.pair_live(4):
                            act.wait_ge(d_ld, st.pair(4))
                            act.activation(le[:, :, :], ld[:, :, :], ACT.Exp).then_inc(e_le, 1)
                        if st.live(6):
                            act.wait_ge(s_x2T, st.at(1, 6, 1))
                            copy(x2T[:, :, :].rearrange("p c q -> p (c q)"), M2[:, 0:DC * S]).then_inc(e_x2T, 1)
                        if st.live(3):
                            act.wait_ge(s_x1T, st.at(1, 3, 1))
                            copy(x1T[:, :, :].rearrange("p c q -> p (c q)"), M1[:, 0:DC * S]).then_inc(e_x1T, 1)
                        if st.live(4):
                            act.wait_ge(d_nm, st.at(1, 4, 1))
                            if st.live(5):
                                act.wait_ge(s_BT, st.at(1, 5, 1))
                            act.activation(pB[:, :], sB[:, :], ACT.Exp, bias=nmB[:, :], scale=0.125,
                                           accum_out=rsB[:, st.par(4):st.par(4) + 1]).then_inc(e_B, 1)
                        if st.live(7):
                            if st.live(9):
                                act.wait_ge(o_row[st.par(7)], st.half_at(9))
                            copy(row[:, st.par(7), 0:D], x2[:, st.par(7), :]).then_inc(e_row, 1)
                    if g == 2:
                        if st.live(3):
                            put_context_values(st)
                            act.wait_ge(s_qh, st.at(1, 3, 1))
                            act.activation(qhT[:, :], M0[0:DK, 0:S], ACT.Identity, bias=xbq[:, :]).then_inc(e_qh, 1)
                    if g == 3:
                        if s == 0 and st.live(0):
                            put_v(st, 0, M1)
                        if st.live(4):
                            act.wait_ge(s_BT, st.at(1, 4, 1))
                            copy(pBT[:, 0:2, :].rearrange("p m q -> p (m q)"), M2[:, 0:2 * S])
                            copy(pBT[0:MT[2][1], 2, :], M2[0:MT[2][1], 2 * S:3 * S]).then_inc(e_BT, 1)
                    if g == 1 and st.live(5):
                        normalise(x2[:, st.par(5), :], z2[:, :], rs2, p_sh2, e_x2, st.at(1, 5, 1),
                                  *[(e_row, st.at(1, 7, 1)), (e_x3, st.at(1, 7, 1))] * st.live(7))
                    if g >= 1 and st.live(0):
                        probabilities(st, 0, g - 1)
                if st.live(4):
                    act.wait_ge(s_o, st.at(1, 4, 1))
                    copy(oT[:, :], M1[0:DK + 1, 0:S]).then_inc(e_o, 1)
                if s == 0 and st.live(-1):
                    if st.live(1):
                        act.wait_ge(s_PV, st.at(Q, 1, Q))
                    put_v(st, -1, M2)
                if s == 1 and st.pair_live(-1):
                    put_q(st.pair(-1))

            turns(act, step)

            def rows_in(n, r):
                act.wait_ge(s_bT, n)
                copy(bxT[:, r, :, :].rearrange("p c t -> p (c t)"), psX[:, 0:DC * CAP]).then_inc(e_bT, 1)

            rows_in(1, 0)

            def expert(v, r, old1, old2, last):
                act.wait_ge(l_w1[r], v * 32 + 32)
                if old2:
                    act.wait_ge(s_y, v * 2 + (r - 1))
                for q in (0, 2):
                    act.wait_ge(s_h, v * 8 + (4 * r + q + 1))
                    if old1:
                        act.wait_ge(d_hl, v * 8 + (4 * r + q - 3))
                    for j in (2 * q, 2 * q + 1):
                        i = act.activation(hT[:, j, :], psH[q][:, (j % 2) * CAP:(j % 2 + 1) * CAP], ACT.Relu,
                                           bias=b1[:, r, j:j + 1])
                    i.then_inc(e_h, 1)
                    act.wait_ge(e_h, v * 4 + (2 * r + q // 2 + 1))
                    copy(hh[:, r, 2 * q:2 * q + 2, :], hT[:, 2 * q:2 * q + 2, :]).then_inc(e_hh, 1)
                    act.wait_ge(d_h, v * 4 + (2 * r + q // 2 + 1))
                    copy(hh[:, r, 2 * q + 2:2 * q + 4, :], hT[:, 2 * q + 2:2 * q + 4, :]).then_inc(e_hh, 1)
                if not last:
                    rows_in(v * 2 + (r + 2), 1 - r)
                act.wait_ge(l_w2[r], v * 16 + 16)
                copy(w2h[:, r, :, :], w2[:, r, :, :]).then_inc(e_w2, 1)

            experts(act, expert)

        @block.vector
        def _(dve):
            def normal_stats(z, stats, moments, s_z, n_z, s_st, s_mv, value):
                dve.wait_ge(s_z, n_z)
                dve.bn_stats(stats, z).then_inc(s_st, 1)
                waits(dve, (s_st, value))
                dve.bn_aggr(moments, stats).then_inc(s_mv, 1)

            dve.memset(kM[:, 0, :, :, :, :].bitcast(F32), 0.0).then_inc(d_zero, 1)
            dve.wait_ge(s_wc, 1)
            dve.tensor_copy(wc[:, :, :].rearrange("p c l -> p (c l)"), M0[:, 0:DC * DL]).then_inc(d_wc, 1)

            def put_latent(p):
                dve.wait_ge(s_lat, p)
                dve.tensor_copy(latT[:, :], M1[0:DL, 0:2 * S]).then_inc(d_lat, 1)

            def put_low_queries(p):
                dve.wait_ge(e_q, p)
                dve.tensor_tensor(ql[:, :, :].rearrange("p c t -> p (c t)"), M2[:, 0:DC * 2 * S],
                                  qh[:, :, :].rearrange("p c t -> p (c t)").bitcast(F32), ALU.subtract).then_inc(d_ql, 1)

            def put_keys(n):
                dve.wait_ge(s_k, n)
                if not isinstance(n, int) or n > 1:
                    for l_ in l_k:
                        dve.wait_ge(l_, n * (16 * HQ) - 16 * HQ)
                keys = M0[:, 0:DC * S].rearrange("p (c t) -> p c t", c=DC)
                dve.tensor_copy(kh, keys).then_inc(d_kh, 1)
                dve.wait_ge(d_kh, n)
                dve.tensor_tensor(kl, keys, kh.bitcast(F32), ALU.subtract).then_inc(d_kl, 1)

            def masked_scores(st):
                waits(dve, (d_msk, 1), (s_B, st.at(1, 4, 1)), *[(e_B, st.at(1, 5, 1))] * st.live(5))
                dve.tensor_tensor_reduce(sB[:, :], M0[0:S, 0:M], msk[:, :], 1.0, -3.0e38, ALU.add, ALU.max,
                                         mxB[:, :]).then_inc(d_B, 1)
                dve.wait_ge(d_B, st.at(1, 4, 1))
                dve.tensor_scalar(nmB[:, :], mxB[:, :], -0.125, None, ALU.mult).then_inc(d_nm, 1)

            def second_residual(st, k):
                dve.wait_ge(e_B, st.at(1, k, 1))
                dve.reciprocal(rvB[:, :], rsB[:, st.par(k):st.par(k) + 1]).then_inc(d_rv, 1)
                dve.wait_ge(d_rv, st.at(1, k, 1))
                dve.wait_ge(s_wo2, st.at(1, k, 1))
                if st.live(k + 1):
                    dve.wait_ge(e_x2, st.at(1, k + 1, 1))
                dve.scalar_tensor_tensor(out=z2[:, :], in0=M1[0:S, 0:D], scalar=rvB[:, :], in1=x1[:, st.par(k), :],
                                         op0=ALU.mult, op1=ALU.add).then_inc(d_z2, 1)

            def second_stats(st, k):
                normal_stats(z2[:, :], st2[:, :], mv2[:, :], d_z2, st.at(1, k, 1), d_st2, d_mv2, st.at(1, k, 1))

            put_latent(1)
            dve.wait_ge(l_w, 16 * N_W)
            put_keys(1)
            put_low_queries(1)
            def put_mask():
                dve.wait_ge(l_late, 16 * N_LATE)
                dve.tensor_scalar(msk[:, :], mski[:, :], 0.0, MASKED, ALU.is_equal, ALU.mult).then_inc(d_msk, 1)

            def step(st):
                s = st.s
                if s == 0 and st.live(4):
                    masked_scores(st)
                for g in range(Q):
                    if g == 1 and s == 1 and st.pair_live(-1):
                        dve.wait_ge(s_v, st.at(1, 0, 1))
                        put_latent(st.pair(-1))
                    if st.live(0):
                        waits(dve, (s_S, st.at(Q, 0, g + 1)), *[(e_exp, st.at(Q, 1, g + 1))] * st.live(1))
                        for j in range(HQ):
                            h = g * HQ + j
                            i = dve.tensor_tensor_reduce(sc[:, h, :], psS[g % 2][0:S, j * S:(j + 1) * S], dec, 1.0, -3.0e38,
                                                         ALU.mult, ALU.max, mx[:, h:h + 1])
                        i.then_inc(d_max, 1)
                    if g == 0 and s == 1 and st.live(4):
                        masked_scores(st)
                    if g == 1 and not st.live(2) and st.live(-1):
                        put_keys(st.at(1, -1, 1))
                    if g == 1 and st.live(2):
                        dve.wait_ge(s_wo, st.at(1, 2, 1))
                        dve.wait_ge(l_xN[st.par(2)], st.half_at(2))
                        if st.live(3):
                            dve.wait_ge(e_x1, st.at(1, 3, 1))
                        dve.tensor_tensor(z1[:, :], M0[0:S, 0:D], xN[:, st.par(2), :], ALU.add).then_inc(d_z1, 1)
                        normal_stats(z1[:, :], st1[:, :], mv1[:, :], d_z1, st.at(1, 2, 1), d_st1, d_mv1, st.at(1, 2, 1))
                        if st.live(-1):
                            put_keys(st.at(1, -1, 1))
                    if g == 2 and st.live(6):
                        dve.wait_ge(s_lg, st.at(1, 6, 1))
                        dve.tensor_tensor(lg[:, s, :], M2[0:S, 0:E], bg[:, :], ALU.add).then_inc(d_lg, 1)
                        if st.live(7):
                            dve.wait_ge(p_sh3, st.at(1, 7, 1))
                        normal_stats(x2[:, s, :], st3[:, :], mv3[:, :], e_x2, st.at(1, 6, 1), d_st3, d_mv3, st.at(1, 6, 1))
                    if g == 2 and s == 0 and st.pair_live(4):
                        dve.wait_ge(s_cum, st.pair(4))
                        dve.tensor_tensor(pose[:, :, :], M2[0:S, E:3 * E].rearrange("p (s e) -> p s e", s=2), oh[:, :, :],
                                          ALU.mult).then_inc(d_pose, 1)
                        dve.tensor_tensor(seen[:, :], seen[:, :], oh[:, 0, :], ALU.add).then_inc(d_seen, 1)
                        dve.wait_ge(d_seen, st.pair(4, 2, 1))
                        dve.tensor_tensor(seen[:, :], seen[:, :], oh[:, 1, :], ALU.add).then_inc(d_seen, 1)
                        dve.wait_ge(d_pose, st.pair(4))
                        dve.tensor_reduce(pos[:, :], pose[:, :, :], AX_X, ALU.add).then_inc(d_pos, 1)
                        dve.wait_ge(d_pos, st.pair(4))
                        dve.tensor_scalar(over[:, :], pos[:, :], float(CAP), FAR, ALU.is_gt, ALU.mult)
                        dve.scalar_tensor_tensor(out=base[:, :], in0=kmax[:, :], scalar=-float(CAP), in1=pos[:, :],
                                                 op0=ALU.mult, op1=ALU.add).then_inc(d_base, 1)
                        dve.wait_ge(d_base, st.pair(4))
                        if st.pair_live(5):
                            for i in range(2):
                                dve.wait_ge(o_row[i], (st.pair(5)) * 16)
                        dve.scalar_tensor_tensor(out=slot[:, :], in0=base[:, :], scalar=float(E * CAP - 1), in1=over[:, :],
                                                 op0=ALU.add, op1=ALU.add).then_inc(d_slot, 1)
                        dve.wait_ge(e_le, st.pair(4))
                        dve.tensor_reduce(den[:, :], le[:, :, :], AX_X, ALU.add).then_inc(d_den, 1)
                        dve.wait_ge(d_den, st.pair(4))
                        dve.wait_ge(e_row, st.pair(4, 2, 2))
                        dve.reciprocal(row[:, :, GATE:GATE + 1], den[:, :].rearrange("p (s o) -> p s o", o=1)).then_inc(d_row, 1)
                        dve.tensor_copy(row[:, :, TOK:TOK + 1],
                                        tok[:, bass.ds(st.batch(8), 2)].rearrange("p (s o) -> p s o", o=1)).then_inc(d_row, 1)
                if st.peeled and st.u == 0 and s == 0:
                    put_mask()
                if s == 0 and st.live(4):
                    second_residual(st, 4)
                if st.live(1):
                    dve.wait_ge(s_PV, st.at(Q, 1, Q))
                    dve.reciprocal(rec[:, :], psO[:, DC * S:2 * DC * S]).then_inc(d_rec, 1)
                    dve.wait_ge(d_rec, st.at(1, 1, 1))
                    if st.live(2):
                        dve.wait_ge(s_wo, st.at(1, 2, 1))
                    dve.tensor_tensor(aT[:, :, :].rearrange("p c q -> p (c q)"), psO[:, 0:DC * S], rec[:, :],
                                      ALU.mult).then_inc(d_aT, 1)
                if s == 1 and st.pair_live(-1):
                    put_low_queries(st.pair(-1))
                if s == 1 and st.live(4):
                    second_residual(st, 4)
                if st.live(4):
                    second_stats(st, 4)
                if s == 1 and st.pair_live(3):
                    dve.wait_ge(d_lg, st.pair(3, 2, 2))
                    dve.tensor_reduce(lmax[:, :], lg[:, :, :], AX_X, ALU.max).then_inc(d_lmax, 1)
                    dve.wait_ge(d_lmax, st.pair(3))
                    dve.tensor_tensor(ld[:, :, :], lg[:, :, :],
                                      lmax[:, :].rearrange("p (s o) -> p s o", o=1).broadcast_to([S, 2, E]),
                                      ALU.subtract).then_inc(d_ld, 1)
                    dve.wait_ge(d_ld, st.pair(3))
                    dve.scalar_tensor_tensor(out=key[:, :, :], in0=ld[:, :, :], scalar=0.0, in1=rev,
                                             op0=ALU.is_ge, op1=ALU.mult).then_inc(d_key, 1)
                    dve.wait_ge(d_key, st.pair(3))
                    dve.tensor_reduce(kmax[:, :], key[:, :, :], AX_X, ALU.max).then_inc(d_kmax, 1)
                    dve.wait_ge(d_kmax, st.pair(3))
                    dve.tensor_tensor(oh[:, :, :], rev,
                                      kmax[:, :].rearrange("p (s o) -> p s o", o=1).broadcast_to([S, 2, E]),
                                      ALU.is_equal).then_inc(d_oh, 1)

            turns(dve, step)

            def expert(v, r, old1, old2, last):
                dve.wait_ge(l_w1[r], v * 32 + 32)
                if old2:
                    dve.wait_ge(s_y, v * 2 + (r - 1))
                for q in (1, 3):
                    dve.wait_ge(s_h, v * 8 + (4 * r + q + 1))
                    if old1:
                        dve.wait_ge(d_hl, v * 8 + (4 * r + q - 3))
                    for j in (2 * q, 2 * q + 1):
                        i = dve.tensor_scalar(hT[:, j, :], psH[q][:, (j % 2) * CAP:(j % 2 + 1) * CAP],
                                              b1[:, r, j:j + 1], 0.0, ALU.add, ALU.max)
                    i.then_inc(d_h, 1)
                    for k in (q - 1, q):
                        dve.wait_ge(e_hh, v * 8 + (4 * r + k + 1))
                        chunk = slice(2 * k, 2 * k + 2)
                        dve.tensor_tensor(hl[:, r, chunk, :], hT[:, chunk, :], hh[:, r, chunk, :].bitcast(F32),
                                          ALU.subtract).then_inc(d_hl, 1)
                dve.wait_ge(e_w2, v * 2 + (r + 1))
                dve.tensor_tensor(w2l[:, r, :, :], w2[:, r, :, :], w2h[:, r, :, :].bitcast(F32), ALU.subtract).then_inc(d_w2, 1)
                if old1:
                    finish(v, r, old2)

            def finish(v, r, more):
                n, k = v * 2 + r, 1 - r
                dve.wait_ge(l_bz[k], v * 32 + 32 * r)
                if more:
                    dve.wait_ge(o_yo[k][1], v * 16 + (16 * r - 16))
                    dve.wait_ge(o_yo[k][0], v * 16 + (16 * r - 16))
                dve.tensor_copy(toki[:, k, :].rearrange("p (i o) -> p i o", o=1), bz[:, k, :, TOK:TOK + 1]).then_inc(d_tok, 1)
                dve.wait_ge(s_y, n)
                if more:
                    dve.wait_ge(d_zf, v * 4 + (2 * r - 2))
                dve.tensor_tensor(yb[:, :, :], psY[k][0:HALF, :].rearrange("p (i d) -> p i d", i=2),
                                  b2[:, k, :].rearrange("p (o d) -> p o d", o=1).broadcast_to([HALF, 2, D]),
                                  ALU.add).then_inc(d_yb, 1)
                dve.wait_ge(d_yb, n)
                if more:
                    dve.wait_ge(p_yo, v * 4 + (2 * r - 2))
                for i in range(2):
                    dve.scalar_tensor_tensor(out=zf[:, i, :], in0=yb[:, i, :], scalar=bz[:, k, i, GATE:GATE + 1],
                                             in1=bz[:, k, i, 0:D], op0=ALU.mult, op1=ALU.add).then_inc(d_zf, 1)
                for i in range(2):
                    dve.wait_ge(d_zf, v * 4 + (2 * r - 1 + i))
                    dve.bn_stats(stf[:, i, :], zf[:, i, :]).then_inc(d_stf, 1)
                for i in range(2):
                    waits(dve, (d_stf, v * 4 + (2 * r - 1 + i)))
                    dve.bn_aggr(mvf[:, i, :], stf[:, i, :]).then_inc(d_mvf, 1)

            experts(dve, expert)
            finish(E // 2, 0, True)

        @block.gpsimd
        def _(pool):
            pool.memset(ones[:, :], 1.0).then_inc(p_set, 1)
            pool.memset(half[:, :], -0.5).then_inc(p_set, 1)
            pool.memset(epst[:, :], EPS).then_inc(p_set, 1)
            pool.memset(seen[:, :], 0.0).then_inc(p_set, 1)
            pool.memset(vS[:, :, :, :], 0.0).then_inc(p_set, 1)
            pool.memset(onesS[:, :, :], 0.0).then_inc(p_set, 1)
            for k in range(2):
                pool.wait_ge(p_set, 6)
                pool.memset(onesS[:, k, k * HD:(k + 1) * HD], 1.0).then_inc(p_set, 1)
            pool.memset(vh[:, :, :, DK:DK + 1], 1.0).then_inc(p_set, 1)
            pool.memset(empty[:, 0:TOK], 0.0).then_inc(p_set, 1)
            pool.memset(empty[:, TOK:ROW], FAR).then_inc(p_set, 1)
            pool.memset(row[:, :, TOK + 1:ROW], 0.0).then_inc(p_row0, 1)
            pool.memset(kM[:, 1, :, :, :, :].bitcast(F32), 0.0).then_inc(p_zero, 1)
            pool.wait_ge(p_set, N_SET)

            def scale_and_shift(mv, ve, rs, s_mv, s_ve, s_rs, s_sh, value, used):
                pool.wait_ge(s_mv, value)
                pool.tensor_tensor(ve[:, :], mv[:, 1:2], epst[0:S, 0:1], ALU.add).then_inc(s_ve, 1)
                pool.wait_ge(s_ve, value)
                if used is not None:
                    pool.wait_ge(used, value - 1)
                pool.tensor_tensor(rs[:, 0:1], ve[:, :], half[0:S, 0:1], ALU.pow).then_inc(s_rs, 1)
                waits(pool, (s_rs, value))
                pool.tensor_scalar(rs[:, 1:2], mv[:, 0:1], rs[:, 0:1], -1.0, ALU.mult, ALU.mult).then_inc(s_sh, 1)

            def dispatch(st):
                waits(pool, (d_row, st.pair(4, 2, 2)), (d_slot, st.pair(4)), (o_empty, 16), (p_row0, 1))
                pool.indirect_dma_start(slots, bass.IndirectOffsetOnAxis(ap=slot[:, st.s:st.s + 1].bitcast(U32), axis=0),
                                        row[:, st.s, :], None, bounds_check=E * CAP - 1,
                                        oob_is_err=False).then_inc(o_row[st.s], 16)

            def step(st):
                s = st.s
                for g in range(Q):
                    if g == 1 and s == 1 and st.pair_live(4):
                        dispatch(st)
                    if st.live(0):
                        pool.wait_ge(d_max, st.at(Q, 0, g + 1))
                        quad = sc[:, g * HQ:(g + 1) * HQ, :]
                        pool.tensor_tensor(quad, quad,
                                           mx[:, g * HQ:(g + 1) * HQ].rearrange("p (h o) -> p h o", o=1).broadcast_to([S, HQ, S]),
                                           ALU.subtract).then_inc(p_sub, 1)
                    if g == 0 and st.live(5):
                        scale_and_shift(mv2, ve2, rs2, d_mv2, p_ve2, p_rs2, p_sh2, st.at(1, 5, 1), e_x2 if st.live(6) else None)
                    if g == 3 and st.live(2):
                        scale_and_shift(mv1, ve1, rs1, d_mv1, p_ve1, p_rs1, p_sh1, st.at(1, 2, 1), e_x1 if st.live(3) else None)
                if st.live(6):
                    scale_and_shift(mv3, ve3, rs3, d_mv3, p_ve3, p_rs3, p_sh3, st.at(1, 6, 1), e_x3 if st.live(7) else None)
                if s == 0 and st.pair_live(4):
                    dispatch(st)

            turns(pool, step)

            out_v = out.rearrange("b s d -> (b s) d")
            for i in range(2):
                pool.wait_ge(o_x3[i], 16 * (B // 2))

            def expert(v, r, old1, old2, last):
                m = v * 4 + 2 * r
                n = v * 2 + (r + 1)
                pool.wait_ge(d_mvf, m + 2)
                pool.tensor_tensor(vef[:, :].rearrange("p (i o) -> p i o", o=1), mvf[:, :, 1:2],
                                   epst[0:HALF, 0:2].rearrange("p (i o) -> p i o", o=1), ALU.add).then_inc(p_vef, 1)
                pool.wait_ge(p_vef, n)
                pool.tensor_tensor(rsf[:, :], vef[:, :], half[0:HALF, 0:2], ALU.pow).then_inc(p_rsf, 1)
                for i in range(2):
                    waits(pool, (p_rsf, n), *[(o_yo[r][i], v * 16)] * old2)
                    pool.tensor_scalar(yo[:, r, i, :], zf[:, i, :], mvf[:, i, 0:1], rsf[:, i:i + 1],
                                       ALU.subtract, ALU.mult).then_inc(p_yo, 1)
                pool.wait_ge(d_tok, n)
                for i in range(2):
                    waits(pool, (p_yo, m + (1 + i)))
                    pool.indirect_dma_start(out_v, bass.IndirectOffsetOnAxis(ap=toki[:, r, i:i + 1].bitcast(U32), axis=0),
                                            yo[:, r, i, :], None, bounds_check=T - 1,
                                            oob_is_err=False).then_inc(o_yo[r][i], 16)

            experts(pool, expert)


def layout(x, ctx_1024, mask_1xSxS2_ik1, L0_attn_W_q, L0_attn_W_k, L0_attn_W_v, L0_attn_W_o, L0_attn_W_down_kv,
           L0_attn_W_up_k, L0_attn_W_up_v, L0_xattn_Wq, L0_xattn_bq, L0_xattn_Wk, L0_xattn_bk, L0_xattn_Wv,
           L0_xattn_bv, L0_xattn_Wo, L0_xattn_bo, L0_ffn_Wg, L0_ffn_bg, L0_ffn_W1, L0_ffn_b1, L0_ffn_W2, L0_ffn_b2):
    r = {
        "x": x, "xT": x.transpose(2, 0, 1).reshape(D, T), "ctxT": ctx_1024.transpose(2, 0, 1).reshape(D, B * M),
        "mask": mask_1xSxS2_ik1[0], "wq": L0_attn_W_q, "wkT": L0_attn_W_k.T, "wvT": L0_attn_W_v.T,
        "wo": L0_attn_W_o.reshape(DC, 2, HQ, HD, D).transpose(0, 2, 1, 3, 4).reshape(D, D), "wd": L0_attn_W_down_kv, "wuk": L0_attn_W_up_k, "wuv": L0_attn_W_up_v,
        "xwqT": L0_xattn_Wq.T, "xbq": L0_xattn_bq[:, None], "xwkT": L0_xattn_Wk.T, "xbk": L0_xattn_bk[:, None],
        "xwvT": L0_xattn_Wv.T, "xbv": L0_xattn_bv[:, None], "xwoT": L0_xattn_Wo.T, "xbo": L0_xattn_bo[None, :],
        "wg": L0_ffn_Wg, "bg": L0_ffn_bg[None, :], "w1": L0_ffn_W1,
        "b1": L0_ffn_b1.reshape(E, HC, P).transpose(0, 2, 1), "w2": L0_ffn_W2, "b2": L0_ffn_b2,
        "cst": constants(),
    }
    return {k: np.ascontiguousarray(v) for k, v in r.items()}


def kernel(**inputs):
    import concourse.bacc as bacc
    from concourse.bass_utils import run_bass_kernel_spmd

    arrays = layout(**{k: np.asarray(v) for k, v in inputs.items()})
    nc = bacc.Bacc("TRN2", target_bir_lowering=False, num_devices=1)
    aps = {k: nc.dram_tensor(f"in_{k}", v.shape, mybir.dt.from_np(v.dtype), kind="ExternalInput").ap()
           for k, v in arrays.items()}
    out = nc.dram_tensor("out_0", (B, S, D), F32, kind="ExternalOutput").ap()
    decoder_kernel(nc, aps, out)
    r = run_bass_kernel_spmd(nc, [{f"in_{k}": v for k, v in arrays.items()}], core_ids=[0])
    return r.results[0]["out_0"]
```
